# Optimizing a Trainium2 kernel written in Bass

```python
import numpy as np
import jax
import jax.numpy as jnp

def _softmax(x, axis=-1):
    return jax.nn.softmax(x, axis=axis)
def _gelu(x):
    return jax.nn.gelu(x, approximate=True)
def _silu(x):
    return jax.nn.silu(x)
def _sigmoid(x):
    return jax.nn.sigmoid(x)
def _layernorm(x, axis=-1, eps=1e-5):
    m = jnp.mean(x, axis=axis, keepdims=True)
    v = jnp.var(x, axis=axis, keepdims=True)
    return (x - m) / jnp.sqrt(v + eps)
def _scatter_add(tgt, idx, src, axis=0):
    return tgt.at[idx].add(src)
def _segment_sum(src, seg, n):
    return jax.ops.segment_sum(src, seg, n)

kernel_name = 'mk_conv_seq_d2_conv_nchw512_594d44'

def setup_inputs(seed: int = 0):
    np.random.seed(seed)
    _w = jnp.asarray
    def _rec_inputs():
        import jax
        import jax.numpy as jnp
        _gk = jax.random.key(seed)
        x = -0.0002928 + 1 * jax.random.normal(jax.random.fold_in(_gk, 1), (8, 512, 32, 32), jnp.float32)
        return x
    x = _rec_inputs()
    def _L0_conv_setup():
        import jax, jax.numpy as jnp
        import numpy as np
        NUM_HEADS = 8
        GN_GROUPS = 8
        GN_EPS = 1e-05
        key = jax.random.key(seed)
        k1, k2, k3 = jax.random.split(key, 3)
        B, C, H, W = (8, 512, 32, 32)
        x = jax.random.normal(k1, (B, C, H, W), dtype=jnp.float32)
        w_qkv = jax.random.normal(k2, (3 * C, C), dtype=jnp.float32) * 0.02
        w_proj = jax.random.normal(k3, (C, C), dtype=jnp.float32) * 0.02
        gamma = jnp.ones((C,), dtype=jnp.float32)
        beta = jnp.zeros((C,), dtype=jnp.float32)
        return {'x': x, 'w_qkv': w_qkv, 'w_proj': w_proj, 'gamma': gamma, 'beta': beta}
    _L0_conv_all = _L0_conv_setup()
    _L0_conv_in = {k: v for k, v in _L0_conv_all.items() if k in ('w_qkv', 'w_proj', 'gamma', 'beta', )}
    del _L0_conv_all

    def _L1_conv_setup():
        import jax, jax.numpy as jnp
        import numpy as np
        NUM_HEADS = 8
        NUM_GROUPS = 8
        EPS = 1e-05

        def group_norm(x, gamma, beta):
            B, C, H, W = x.shape
            xg = x.reshape(B, NUM_GROUPS, C // NUM_GROUPS, H, W)
            mean = xg.mean(axis=(2, 3, 4), keepdims=True)
            var = xg.var(axis=(2, 3, 4), keepdims=True)
            xn = ((xg - mean) * jax.lax.rsqrt(var + EPS)).reshape(B, C, H, W)
            return xn * gamma[None, :, None, None] + beta[None, :, None, None]

        def conv1x1(x, w, b):
            return jnp.einsum('oc,bchw->bohw', w, x) + b[None, :, None, None]
        key = jax.random.key(seed)
        ks = jax.random.split(key, 6)
        B, C, H, W = (16, 512, 32, 32)
        x = jax.random.normal(ks[0], (B, C, H, W), dtype=jnp.float32)
        norm_w = jnp.ones((C,), jnp.float32)
        norm_b = jnp.zeros((C,), jnp.float32)
        s = 1.0 / np.sqrt(C)
        qkv_w = jax.random.uniform(ks[1], (3 * C, C), jnp.float32, -s, s)
        qkv_b = jax.random.uniform(ks[2], (3 * C,), jnp.float32, -s, s)
        proj_w = jax.random.uniform(ks[3], (C, C), jnp.float32, -s, s)
        proj_b = jax.random.uniform(ks[4], (C,), jnp.float32, -s, s)
        return {'x': x, 'norm_w': norm_w, 'norm_b': norm_b, 'qkv_w': qkv_w, 'qkv_b': qkv_b, 'proj_w': proj_w, 'proj_b': proj_b}
    _L1_conv_all = _L1_conv_setup()
    _L1_conv_in = {k: v for k, v in _L1_conv_all.items() if k in ('norm_w', 'norm_b', 'qkv_w', 'qkv_b', 'proj_w', 'proj_b', )}
    del _L1_conv_all

    return {
        "x": x,
        "L0_conv_w_qkv": _L0_conv_in["w_qkv"],
        "L0_conv_w_proj": _L0_conv_in["w_proj"],
        "L0_conv_gamma": _L0_conv_in["gamma"],
        "L0_conv_beta": _L0_conv_in["beta"],
        "L1_conv_norm_w": _L1_conv_in["norm_w"],
        "L1_conv_norm_b": _L1_conv_in["norm_b"],
        "L1_conv_qkv_w": _L1_conv_in["qkv_w"],
        "L1_conv_qkv_b": _L1_conv_in["qkv_b"],
        "L1_conv_proj_w": _L1_conv_in["proj_w"],
        "L1_conv_proj_b": _L1_conv_in["proj_b"],
    }

def reference(x, L0_conv_w_qkv, L0_conv_w_proj, L0_conv_gamma, L0_conv_beta, L1_conv_norm_w, L1_conv_norm_b, L1_conv_qkv_w, L1_conv_qkv_b, L1_conv_proj_w, L1_conv_proj_b):
    import jax
    import jax.numpy as jnp
    def _L0_conv_ref(x, w_qkv, w_proj, gamma, beta):
        import jax, jax.numpy as jnp
        import numpy as np
        NUM_HEADS = 8
        GN_GROUPS = 8
        GN_EPS = 1e-05
        B, C, H, W = x.shape
        nh = NUM_HEADS
        hd = C // nh
        N = H * W
        scale = jnp.asarray(hd, x.dtype) ** (-0.5)
        xf = x.reshape(B, C, N)
        qkv = jnp.einsum('oc,bcn->bon', w_qkv, xf)
        qkv = qkv.reshape(B, 3, nh, hd, N)
        q, k, v = (qkv[:, 0], qkv[:, 1], qkv[:, 2])
        attn = jnp.einsum('bhdn,bhdm->bhnm', q, k) * scale
        attn = jax.nn.softmax(attn, axis=-1)
        out = jnp.einsum('bhnm,bhdm->bhdn', attn, v)
        out = out.reshape(B, C, N)
        out = jnp.einsum('oc,bcn->bon', w_proj, out).reshape(B, C, H, W)
        g = GN_GROUPS
        og = out.reshape(B, g, C // g, H, W)
        mean = og.mean(axis=(2, 3, 4), keepdims=True)
        var = og.var(axis=(2, 3, 4), keepdims=True)
        normed = ((og - mean) * jax.lax.rsqrt(var + GN_EPS)).reshape(B, C, H, W)
        normed = normed * gamma[None, :, None, None] + beta[None, :, None, None]
        return normed + x

    def _L1_conv_ref(x, norm_w, norm_b, qkv_w, qkv_b, proj_w, proj_b):
        import jax, jax.numpy as jnp
        import numpy as np
        NUM_HEADS = 8
        NUM_GROUPS = 8
        EPS = 1e-05

        def group_norm(x, gamma, beta):
            B, C, H, W = x.shape
            xg = x.reshape(B, NUM_GROUPS, C // NUM_GROUPS, H, W)
            mean = xg.mean(axis=(2, 3, 4), keepdims=True)
            var = xg.var(axis=(2, 3, 4), keepdims=True)
            xn = ((xg - mean) * jax.lax.rsqrt(var + EPS)).reshape(B, C, H, W)
            return xn * gamma[None, :, None, None] + beta[None, :, None, None]

        def conv1x1(x, w, b):
            return jnp.einsum('oc,bchw->bohw', w, x) + b[None, :, None, None]
        B, C, H, W = x.shape
        hd = C // NUM_HEADS
        h = group_norm(x, norm_w, norm_b)
        qkv = conv1x1(h, qkv_w, qkv_b)
        q, k, v = jnp.split(qkv, 3, axis=1)
        q = q.reshape(B, NUM_HEADS, hd, H * W)
        k = k.reshape(B, NUM_HEADS, hd, H * W)
        v = v.reshape(B, NUM_HEADS, hd, H * W)
        scale = hd ** (-0.5)
        attn = jax.nn.softmax(jnp.einsum('bhci,bhcj->bhij', q, k) * scale, axis=-1)
        h = jnp.einsum('bhij,bhcj->bhci', attn, v).reshape(B, C, H, W)
        h = conv1x1(h, proj_w, proj_b)
        return x + h

    def _gn(v, G=32, eps=1e-5):
        B_, C_, H_, W_ = v.shape
        g = v.reshape(B_, G, C_ // G, H_, W_)
        m = jnp.mean(g, axis=(2, 3, 4), keepdims=True)
        s = jnp.var(g, axis=(2, 3, 4), keepdims=True)
        return ((g - m) / jnp.sqrt(s + eps)).reshape(v.shape)

    def _ln_c(v, eps=1e-6):
        m = jnp.mean(v, axis=1, keepdims=True)
        s = jnp.var(v, axis=1, keepdims=True)
        return (v - m) / jnp.sqrt(s + eps)

    def _ln_t(v, eps=1e-5):
        m = jnp.mean(v, axis=-1, keepdims=True)
        s = jnp.var(v, axis=-1, keepdims=True)
        return (v - m) / jnp.sqrt(s + eps)

    def _to_tokens(v):
        B_, C_, H_, W_ = v.shape
        return v.reshape(B_, C_, H_ * W_).transpose(0, 2, 1)
    def _from_tokens(t, like):
        B_, C_, H_, W_ = like.shape
        return t.transpose(0, 2, 1).reshape(B_, C_, H_, W_)

    x = _L0_conv_ref(x, L0_conv_w_qkv, L0_conv_w_proj, L0_conv_gamma, L0_conv_beta)
    x = _L1_conv_ref(x, L1_conv_norm_w, L1_conv_norm_b, L1_conv_qkv_w, L1_conv_qkv_b, L1_conv_proj_w, L1_conv_proj_b)
    return x


_drawn_inputs = setup_inputs


def setup_inputs(seed=0):
    import zlib

    import numpy as np

    out = dict(_drawn_inputs(seed))
    spreads = {'L0_conv_gamma': (1.0, 0.2),
     'L0_conv_beta': (0.0, 0.1),
     'L1_conv_norm_w': (1.0, 0.2),
     'L1_conv_norm_b': (0.0, 0.381)}
    factors = {'L1_conv_qkv_b': 5.272, 'L1_conv_proj_b': 3.163}
    for name, (base, spread) in spreads.items():
        noise = np.random.default_rng([zlib.crc32(name.encode()), seed]).standard_normal(out[name].shape)
        drawn = base * np.exp(spread * noise) if base else spread * noise
        out[name] = jnp.asarray(drawn.astype(out[name].dtype))
    for name, factor in factors.items():
        out[name] = (out[name] * factor).astype(out[name].dtype)
    return out
```

```python
from contextlib import ExitStack

import concourse.bass as bass
from concourse import mybir

F32 = mybir.dt.float32
F16 = mybir.dt.float16
ALU = mybir.AluOpType
ACT = mybir.ActivationFunctionType
AX = mybir.AxisListType

P = 128
HALF = 64
COLS = 512
EPS = 1e-5
WEIGHT_SCALE = 16.0
SHIFT_UNIT = 1024.0
HEADROOM = 256.0


class Tally:

    def __init__(self, sem, lead, per, batches):
        self.sem = sem
        self.lead, self.per = lead, per
        self.start = [0]
        for a, b in zip(lead, per):
            self.start.append(self.start[-1] + a + batches * b)

    def at_lead(self, layer, n):
        return self.start[layer] + n

    def at(self, layer, i, n):
        return self.start[layer] + self.lead[layer] + i * self.per[layer] + n


QK_SLOTS = {3: (0, 0), 4: (0, 1), 5: (1, 0), 6: (1, 1), 7: (2, 0), 8: (2, 1), 9: (3, 0), 10: (3, 1)}
QK_EVICT = {5: 0, 7: 1, 9: 2, 11: 3}
TURN_SLOTS = {11: 0, 12: 1}
TURN_EVICT = {12: 0, 13: 1}
SHIFT_B_CHAIN, SHIFT_B_SLOT, SHIFT_B_COPY = 12, 13, 14
V_START = (14, 21)
V_LONG = 7
V_EVICT = {21: 0, 28: 1}
SHIFT_A_CHAIN, SHIFT_A_SLOT, SHIFT_A_COPY = 28, 29, 30
PV_OFFSETS = {1: 0, 3: 1, 5: 2, 6: 3}
NEXT_X_PAIR, NEXT_X_SLOT = 2, 28


def max_tiles(t):
    if t < 12:
        return [(1, 0, t + 4)]
    if 14 <= t < 28:
        n = t - 14
        first = n + min(n, 2)
        return [(0, 1, first)] + ([(0, 1, first + 1)] if n < 2 else [])
    if t >= 28:
        return [(1, 1, t - 28)]
    return []


def two_attention_blocks(
    nc: bass.Bass,
    x, w_qkv0, w_proj0, gamma0, beta0, norm_w1, norm_b1, w_qkv1, qkv_b1, w_proj1, proj_b1,
    out,
):
    NB, C, N = x.shape
    CT = C // P
    PAIRS = C // P
    HEADS = 2 * PAIRS
    MT = N // P
    NH = N // COLS
    QT = COLS // P
    WCOLS = 4 * C
    SLOTS = 2 * NH * MT
    BSLOTS = PAIRS * SLOTS
    UNITS = 2 * NH * PAIRS
    GROUP = 64
    EXP_SCALE = float(HALF) ** -0.5 / WEIGHT_SCALE ** 2
    VW = 136
    VL = 72
    import math
    SHIFT_BONUS = math.log(HEADROOM) / EXP_SCALE / SHIFT_UNIT
    assert (CT, PAIRS, MT, NH, SLOTS) == (4, 4, 8, 2, 32)

    def item_list(layer):
        items = []
        for p in range(PAIRS):
            items += [("qk", p, 0), ("qk", p, 1), ("qk", p, 2), ("qk", p, 3)]
            if p:
                items += [("turn", p - 1, 0), ("turn", p - 1, 1)]
            items += [("shift", p, 1), ("v", p, 0), ("v", p, 1), ("shift", p, 0)]
        items += [("turn", PAIRS - 1, 0), ("turn", PAIRS - 1, 1)]
        items += [("proj", ot, nh) for ot in range(CT) for nh in range(NH)]
        if layer == 0:
            items += [("norm", 0, 0), ("norm", 1, 0)]
        return items

    ITEMS = [{it: n for n, it in enumerate(item_list(layer))} for layer in range(2)]
    LEAD_ITEMS = {("qk", 0): 0, ("qk", 1): 1, ("qk", 2): 2, ("qk", 3): 3, ("v", 0): 4, ("v", 1): 5, ("shift", 0): 6}
    HIGHS = [{it: n for n, it in enumerate(i for i in item_list(layer) if i[0] in ("qk", "turn", "v", "proj"))}
             for layer in range(2)]
    DVE_LINKS = [0, 0]

    with ExitStack() as ctx:
        def sb(name, shape, dt):
            return ctx.enter_context(nc.sbuf_tensor(name, shape, dt))

        def bank(name):
            return ctx.enter_context(nc.psum_tensor(name, [P, COLS], F32))

        def tally(name, lead, per):
            lead = list(lead) if isinstance(lead, (list, tuple)) else [lead, lead]
            per = list(per) if isinstance(per, (list, tuple)) else [per, per]
            return Tally(ctx.enter_context(nc.semaphore(name)), lead, per, NB)

        y_dram = nc.dram_tensor("y_scratch", (NB, C, N), F32, kind="Internal").ap()

        w_hi = sb("w_hi", [P, CT, WCOLS], F16)
        w_lo = sb("w_lo", [P, CT, WCOLS], F16)
        x_in = sb("x_in", [P, CT, N], F32)
        x_res = sb("x_res", [P, CT, N], F32)
        w_in = x_res[:, :, :].rearrange("p (a b) n -> p a (b n)", a=2)
        x_hi = sb("x_hi", [P, CT, N], F16)
        x_lo = sb("x_lo", [P, CT, N], F16)
        qa = sb("qa", [P, 2, 2, N], F16)
        qb = sb("qb", [P, 2, 2, N], F16)
        ka = sb("ka", [P, 2, 2, N], F16)
        kb = sb("kb", [P, 2, 2, N], F16)
        v = sb("v", [P, 2, MT, 2, VW], F16)
        p_f32 = sb("p_f32", [P, 2, 2, COLS], F32)
        p_hi = sb("p_hi", [P, 2, MT, COLS], F16)
        p_lo = sb("p_lo", [P, 2, MT, COLS], F16)
        o_pair = sb("o_pair", [P, MT, P], F32)
        o_hi = sb("o_hi", [P, CT, N], F16)
        o_lo = sb("o_lo", [P, CT, N], F16)
        yb = sb("yb", [P, CT, N], F32)
        ident = sb("ident", [P, P], F32)
        ident16 = sb("ident16", [P, P], F16)
        group_mean = sb("group_mean", [P, P], F32)
        biases = sb("biases", [P, 2, 4 * CT], F32)
        affine = sb("affine", [P, 4, CT], F32)
        maxes = sb("maxes", [P, 2, 2 * MT], F32)
        row_max = sb("row_max", [P, 2, MT], F32)
        shift = sb("shift", [P, 2, MT], F16)
        shift_rows = sb("shift_rows", [MT, 2, P], F16)
        recip = sb("recip", [P, 2, QT], F32)
        bn = sb("bn", [P, CT, NH, 6], F32)
        mv = sb("mv", [P, CT, 2], F32)
        gs = sb("gs", [P, 2 * CT], F32)
        gm = sb("gm", [P, 2 * CT], F32)
        var = sb("var", [P, CT], F32)
        rstd = sb("rstd", [P, CT], F32)
        tmp = sb("tmp", [P, CT], F32)
        minus_half = sb("minus_half", [P, CT], F32)
        norm_a = sb("norm_a", [P, CT], F32)
        norm_b = sb("norm_b", [P, CT], F32)
        next_a = sb("next_a", [P, NB, CT], F32)
        next_b = sb("next_b", [P, NB, CT], F32)

        s_bank = [bank("s_bank0"), bank("s_bank1")]
        m_bank = [bank("m_bank0"), bank("m_bank1")]
        o_bank = [bank("o_bank0"), bank("o_bank1")]
        g_bank = [bank("g_bank0"), bank("g_bank1")]

        const_ready = ctx.enter_context(nc.semaphore("const_ready"))
        const_step = ctx.enter_context(nc.semaphore("const_step"))
        params_in = ctx.enter_context(nc.semaphore("params_in"))
        params_ready = ctx.enter_context(nc.semaphore("params_ready"))

        N_MAX = HEADS * 2 * MT
        w_loaded = [tally(f"w_loaded{k}", 32, 0) for k in range(CT)]
        w_high = tally("w_high", CT, 0)
        w_low = tally("w_low", CT, 0)
        x_loaded = tally("x_loaded", 16 * CT, 16 * CT)
        x_normed = tally("x_normed", (0, CT), (0, CT))
        x_high = tally("x_high", CT, CT)
        x_low = tally("x_low", CT, CT)
        g_made = tally("g_made", 7, [len(i) for i in ITEMS])
        g_free = tally("g_free", 7, [len(i) for i in ITEMS])
        g_high = tally("g_high", 6, [len(i) for i in HIGHS])
        q_copied = tally("q_copied", 32, 32 * PAIRS)
        k_copied = tally("k_copied", 32, 32 * PAIRS)
        max_made = tally("max_made", 20, N_MAX)
        max_read = tally("max_read", 20, N_MAX)
        max_joined = tally("max_joined", 1, HEADS)
        shift_ready = tally("shift_ready", 1, HEADS)
        shift_placed = tally("shift_placed", 16, 16 * HEADS)
        s_made = tally("s_made", 0, BSLOTS)
        p_made = tally("p_made", 0, BSLOTS)
        p_rest = tally("p_rest", 0, BSLOTS // 2)
        o_made = tally("o_made", 0, UNITS)
        o_recip = tally("o_recip", 0, UNITS)
        o_read = tally("o_read", 0, UNITS)
        res_loaded = tally("res_loaded", 0, 16 * CT)
        res_added = tally("res_added", (1, 0), [CT, CT * NH])
        y_scaled = tally("y_scaled", 0, [CT, 0])
        y_stored = tally("y_stored", (1, 0), 16 * CT)
        stats_ready = tally("stats_ready", 0, [2, 0])
        var_ready = tally("var_ready", 0, [2, 0])
        rstd_ready = tally("rstd_ready", 0, [2, 0])
        norm_ready = tally("norm_ready", 0, [2, 0])
        links = tally("links", 0, [2 * 6 + 1, 0])

        block = ctx.enter_context(nc.Block())

        def own(h):
            return slice(h * HALF, (h + 1) * HALF)

        def other_row(h):
            return HALF if h == 0 else 0

        def lead_at(layer):
            return lambda t, n: t.at_lead(layer, n)

        def batch_at(layer, i):
            return lambda t, n: t.at(layer, i, n)

        def bank_of(layer, n, lead=False):
            first = sum(7 + NB * len(ITEMS[k]) for k in range(layer)) + (0 if lead else 7)
            return g_bank[(first + n) % 2]

        @block.sync
        def _(sp):
            def copy_q(at, p1, st):
                n = at(g_high, p1)
                sp.wait_ge(g_high.sem, n)
                for h in range(2):
                    sp.dma_start(qa[own(1 - h), st, h, :], qa[own(h), st, h, :]).then_inc(q_copied.sem, 16)

            def copy_k(at, p1, st):
                sp.wait_ge(g_high.sem, at(g_high, p1))
                for h in range(2):
                    sp.dma_start(kb[own(h), st, h, :], ka[own(h), st, h, :]).then_inc(k_copied.sem, 16)

            def place_shift(at, n_item, n_row, st, h):
                del n_row
                sp.wait_ge(g_free.sem, at(g_free, n_item + 1))
                r = other_row(h)
                sp.dma_start(qb[r:r + 1, st, h, :].rearrange("o (a n) -> o a n", a=MT), shift_rows[:, h, :])\
                    .then_inc(shift_placed.sem, 16)

            def load_x(at, source, index):
                for kt in range(CT):
                    sp.dma_start(x_in[:, kt, :], source[index, kt * P:(kt + 1) * P, :].rearrange("b p n -> p (b n)"))\
                        .then_inc(x_loaded.sem, 16)

            sp.dma_start(biases[:, 1, 0:3 * CT], qkv_b1).then_inc(params_in, 16)
            sp.dma_start(biases[:, 1, 3 * CT:4 * CT], proj_b1).then_inc(params_in, 16)
            for n, a in enumerate((gamma0, beta0, norm_w1, norm_b1)):
                sp.dma_start(affine[:, n, :], a).then_inc(params_in, 16)
            for layer in range(2):
                wq, wp = ((w_qkv0, w_proj0), (w_qkv1, w_proj1))[layer]
                source = (x, y_dram)[layer]
                target = (y_dram, out)[layer]
                at = lead_at(layer)
                if layer == 1:
                    sp.wait_ge(res_added.sem, at(res_added, 0))
                for kt in range(CT):
                    if kt >= 2:
                        sp.wait_ge(w_low.sem, at(w_low, kt - 1))
                    sp.dma_start(w_in[:, kt % 2, 0:3 * C], wq[kt * P:(kt + 1) * P, :]).then_inc(w_loaded[kt].sem, 16)
                    sp.dma_start(w_in[:, kt % 2, 3 * C:4 * C], wp[kt * P:(kt + 1) * P, :]).then_inc(w_loaded[kt].sem, 16)
                if layer == 1:
                    sp.wait_ge(y_stored.sem, at(y_stored, 0))
                    sp.wait_ge(x_low.sem, at(x_low, 0))
                load_x(at, source, slice(0, 1))
                copy_q(at, 2, 0)
                copy_k(at, 4, 0)
                place_shift(at, LEAD_ITEMS["shift", 0], 0, 0, 0)

                with sp.Fori(0, NB) as i:
                    at = batch_at(layer, i)
                    following = bass.ds((i + 1) % NB, 1)
                    sp.wait_ge(x_low.sem, at(x_low, 0))
                    load_x(at, source, following)
                    for p in range(PAIRS):
                        st = (p + 1) % 2
                        copy_q(at, HIGHS[layer]["qk", p, 1] + 1, st)
                        copy_k(at, HIGHS[layer]["qk", p, 3] + 1, st)
                        place_shift(at, ITEMS[layer]["shift", p, 1], 0, p % 2, 1)
                        place_shift(at, ITEMS[layer]["shift", p, 0], 0, st, 0)
                        if p == 1:
                            sp.wait_ge(res_added.sem, at(res_added, 0))
                            if layer == 0:
                                sp.wait_ge(w_low.sem, w_low.at_lead(0, CT))
                            for ot in range(CT):
                                sp.dma_start(x_res[:, ot, :],
                                             source[bass.ds(i, 1), ot * P:(ot + 1) * P, :].rearrange("b p n -> p (b n)"))\
                                    .then_inc(res_loaded.sem, 16)
                    for ot in range(CT):
                        sp.wait_ge(res_added.sem, at(res_added, (ot + 1) * res_added.per[layer] // CT))
                        sp.dma_start(target[bass.ds(i, 1), ot * P:(ot + 1) * P, :].rearrange("b p n -> p (b n)"), yb[:, ot, :])\
                            .then_inc(y_stored.sem, 16)
            sp.wait_ge(y_stored.sem, y_stored.start[2])
            for t in (q_copied, k_copied, shift_placed):
                sp.wait_ge(t.sem, t.start[2])

        @block.gpsimd
        def _(pool):
            steps = [0]

            def step(ins):
                steps[0] += 1
                ins.then_inc(const_step, 1)
                pool.wait_ge(const_step, steps[0])

            for m in (ident, ident16):
                step(pool.memset(m[:, :], 0.0))
                step(pool.affine_select(out=m[:, :], in_=m[:, :], compare_op=ALU.not_equal, fill=1.0, base=0,
                                        pattern=[[-1, P]], channel_multiplier=1))
            step(pool.memset(group_mean[:, :], 0.0))
            for g in range(P // GROUP):
                step(pool.memset(group_mean[g * GROUP:(g + 1) * GROUP, g * GROUP:(g + 1) * GROUP], 1.0 / GROUP))
            for h in range(2):
                r = other_row(h)
                step(pool.memset(kb[own(1 - h), :, h, :], 0.0))
                step(pool.memset(kb[r:r + 1, :, h, :], SHIFT_UNIT))
                step(pool.memset(qb[own(1 - h), :, h, :], 0.0))
            for st in range(2):
                step(pool.memset(v[:, st, :, :, HALF:HALF + 1], 1.0))
            step(pool.memset(biases[:, 0, :], 0.0))
            pool.memset(minus_half[:, :], -0.5).then_inc(const_ready, 1)

            pool.wait_ge(const_ready, 1)
            with pool.Fori(0, NB) as i:
                at = batch_at(0, i)
                for which in range(2):
                    pool.wait_ge(var_ready.sem, at(var_ready, which + 1))
                    pool.tensor_tensor(rstd[:, :], var[:, :], minus_half[:, :], ALU.pow).then_inc(rstd_ready.sem, 1)

        @block.tensor
        def _(pe):
            def split_product(bank_ap, terms, k0=0, k1=None):
                k1 = len(terms) if k1 is None else k1
                for n in range(k0, k1):
                    a, b = terms[n]
                    last = pe.matmul(bank_ap, a, b, start=(n == 0), stop=(n == len(terms) - 1))
                return last

            def claim(at, n):
                pe.wait_ge(g_free.sem, at(g_free, n - 1))

            def qk_terms(p, which):
                w0 = (which // 2) * C + p * P
                cols = slice((which % 2) * COLS, (which % 2 + 1) * COLS)
                terms = []
                for kt in range(CT):
                    wh, wl = w_hi[:, kt, w0:w0 + P], w_lo[:, kt, w0:w0 + P]
                    terms += [(wh, x_hi[:, kt, cols]), (wh, x_lo[:, kt, cols]), (wl, x_hi[:, kt, cols])]
                return terms

            def v_terms(p, mt):
                w0 = 2 * C + p * P
                rows = slice(mt * P, (mt + 1) * P)
                terms = []
                for kt in range(CT):
                    wh, wl = w_hi[:, kt, w0:w0 + P], w_lo[:, kt, w0:w0 + P]
                    terms += [(x_hi[:, kt, rows], wh), (x_hi[:, kt, rows], wl), (x_lo[:, kt, rows], wh)]
                return terms

            def qk_part(g, p, which, part, parts):
                terms = qk_terms(p, which)
                k = len(terms) // parts
                last = split_product(g[:, :], terms, part * k, (part + 1) * k)
                if part == parts - 1:
                    last.then_inc(g_made.sem, 1)

            def v_part(g, p, group, part, parts):
                flat = [(j, n) for j in range(4) for n in range(3 * CT)]
                k0, k1 = part * len(flat) // parts, (part + 1) * len(flat) // parts
                for j, n in flat[k0:k1]:
                    a, b = v_terms(p, 4 * group + j)[n]
                    last = pe.matmul(g[:, j * P:(j + 1) * P], a, b, start=(n == 0), stop=(n == 3 * CT - 1))
                if part == parts - 1:
                    last.then_inc(g_made.sem, 1)

            def max_tile(at, n, st, h, k):
                pe.wait_ge(max_read.sem, at(max_read, n - 1))
                nt, mh = k // 2, k % 2
                pe.matmul(m_bank[n % 2][:, :], qa[:, st, h, nt * P:(nt + 1) * P], ka[:, st, h, mh * COLS:(mh + 1) * COLS],
                          start=True, stop=True).then_inc(max_made.sem, 1)

            def turn_shift(at, g, n_item, n_shift, h):
                claim(at, n_item)
                pe.wait_ge(shift_ready.sem, at(shift_ready, n_shift + 1))
                pe.transpose(g[0:MT, 0:HALF].bitcast(F16), shift[:, h, :], ident16[:, :]).then_inc(g_made.sem, 1)

            def turn_output(at, layer, p, half):
                n = ITEMS[layer]["turn", p, half]
                g = bank_of(layer, n)
                claim(at, n)
                pe.wait_ge(o_read.sem, at(o_read, 4 * (p + 1)))
                for j in range(QT):
                    last = pe.transpose(g[:, j * P:(j + 1) * P], o_pair[:, half * QT + j, :], ident[:, :])
                last.then_inc(g_made.sem, 1)

            def scores(at, T):
                p, h, nh, mt = T // SLOTS, (T % SLOTS) // (NH * MT), (T // MT) % NH, T % MT
                st = p % 2
                s = s_bank[T % 2]
                if T >= 2:
                    pe.wait_ge(p_made.sem, at(p_made, T - 1))
                if T % (NH * MT) == 0:
                    pe.wait_ge(shift_placed.sem, at(shift_placed, 16 * (T // (NH * MT))))
                if T % SLOTS == 0:
                    pe.wait_ge(k_copied.sem, at(k_copied, 32 * p))
                keys, queries = slice(mt * P, (mt + 1) * P), slice(nh * COLS, (nh + 1) * COLS)
                pe.matmul(s[:, :], ka[:, st, h, keys], qa[:, st, h, queries], start=True, stop=False)
                pe.matmul(s[:, :], kb[:, st, h, keys], qb[:, st, h, queries], start=False, stop=True)\
                    .then_inc(s_made.sem, 1)

            def weighted_sum(at, layer, u, k):
                p, h = u // 4, (u // 2) % 2
                st, buf = p % 2, u % 2
                o = o_bank[buf]
                if k == 0:
                    pe.wait_ge(p_rest.sem, at(p_rest, 4 * (u + 1)))
                    if u >= 2:
                        pe.wait_ge(o_read.sem, at(o_read, u - 1))
                    if u % 4 == 0:
                        pe.wait_ge(g_free.sem, at(g_free, 0 if p == 0 else ITEMS[layer]["v", p - 1, 1] + 1))
                for mt in range(MT):
                    hi = p_hi[:, buf, mt, k * P:(k + 1) * P]
                    lo = p_lo[:, buf, mt, k * P:(k + 1) * P]
                    c = k * (HALF + 1)
                    pe.matmul(o[:, c:c + HALF + 1], hi, v[:, st, mt, h, 0:HALF + 1], start=(mt == 0), stop=False)
                    pe.matmul(o[:, c:c + HALF], hi, v[:, st, mt, h, VL:VL + HALF], start=False, stop=False)
                    last = pe.matmul(o[:, c:c + HALF + 1], lo, v[:, st, mt, h, 0:HALF + 1], start=False,
                                     stop=(mt == MT - 1))
                if k == QT - 1:
                    last.then_inc(o_made.sem, 1)

            def project(at, layer, ot, nh):
                n = ITEMS[layer]["proj", ot, nh]
                claim(at, n)
                w0 = 3 * C + ot * P
                cols = slice(nh * COLS, (nh + 1) * COLS)
                terms = []
                for ct in range(CT):
                    wh, wl = w_hi[:, ct, w0:w0 + P], w_lo[:, ct, w0:w0 + P]
                    terms += [(wh, o_hi[:, ct, cols]), (wh, o_lo[:, ct, cols]), (wl, o_hi[:, ct, cols])]
                split_product(bank_of(layer, n)[:, :], terms).then_inc(g_made.sem, 1)

            pe.wait_ge(const_ready, 1)
            for layer in range(2):
                at = lead_at(layer)
                pe.wait_ge(w_low.sem, at(w_low, CT))
                pe.wait_ge(x_low.sem, at(x_low, CT))
                for which in range(4):
                    if which >= 2 or layer:
                        claim(at, which)
                    qk_part(bank_of(layer, which, True), 0, which, 0, 1)
                for group in range(2):
                    claim(at, 4 + group)
                    v_part(bank_of(layer, 4 + group, True), 0, group, 0, 1)
                pe.wait_ge(q_copied.sem, at(q_copied, 32))
                for k in range(20):
                    if k >= 2:
                        max_tile(at, k, 0, k // 16, k % 16)
                    else:
                        pe.matmul(m_bank[k % 2][:, :], qa[:, 0, 0, 0:P], ka[:, 0, 0, k * COLS:(k + 1) * COLS],
                                  start=True, stop=True).then_inc(max_made.sem, 1)
                turn_shift(at, bank_of(layer, 6, True), 6, 0, 0)

                with pe.Fori(0, NB) as i:
                    at = batch_at(layer, i)
                    n_max = 0
                    for T in range(BSLOTS):
                        p, t = T // SLOTS, T % SLOTS
                        st1 = (p + 1) % 2
                        p1 = (p + 1) % PAIRS
                        scores(at, T)
                        if p == PAIRS - 1 and t == 3:
                            pe.wait_ge(x_low.sem, at(x_low, CT))
                        if t == 14:
                            pe.wait_ge(q_copied.sem, at(q_copied, 32 * (p + 1)))
                            pe.wait_ge(g_free.sem, at(g_free, ITEMS[layer]["qk", p, 3] + 1))
                        for h, ahead, k in max_tiles(t):
                            max_tile(at, n_max, st1 if ahead else p % 2, h, k)
                            n_max += 1
                        if t in QK_SLOTS:
                            which, part = QK_SLOTS[t]
                            n = ITEMS[layer]["qk", p, which]
                            if part == 0:
                                claim(at, n)
                            qk_part(bank_of(layer, n), p1, which, part, 2)
                        if t in TURN_SLOTS and p:
                            turn_output(at, layer, p - 1, TURN_SLOTS[t])
                        for h, slot in ((1, SHIFT_B_SLOT), (0, SHIFT_A_SLOT)):
                            if t == slot:
                                n = ITEMS[layer]["shift", p, h]
                                turn_shift(at, bank_of(layer, n), n, 2 * p + 1 - h, h)
                        for group in range(2):
                            if V_START[group] <= t < V_START[group] + V_LONG:
                                n = ITEMS[layer]["v", p, group]
                                if t == V_START[group]:
                                    claim(at, n)
                                v_part(bank_of(layer, n), p1, group, t - V_START[group], V_LONG)
                        if T >= MT and T % MT in PV_OFFSETS:
                            weighted_sum(at, layer, T // MT - 1, PV_OFFSETS[T % MT])
                    assert n_max == N_MAX
                    for k in range(QT):
                        weighted_sum(at, layer, UNITS - 1, k)
                    for half in range(2):
                        turn_output(at, layer, PAIRS - 1, half)
                    pe.wait_ge(g_free.sem, at(g_free, ITEMS[layer]["turn", PAIRS - 1, 1] + 1))
                    for ot in range(CT):
                        for nh in range(NH):
                            project(at, layer, ot, nh)
                    if layer == 0:
                        for which in range(2):
                            n = ITEMS[layer]["norm", which, 0]
                            claim(at, n)
                            pe.wait_ge(stats_ready.sem, at(stats_ready, which + 1))
                            pe.matmul(bank_of(layer, n)[:, 0:2 * CT], group_mean[:, :], gs[:, :], start=True, stop=True)\
                                .then_inc(g_made.sem, 1)

        @block.scalar
        def _(act):
            def made(at, n):
                act.wait_ge(g_made.sem, at(g_made, n + 1))

            def qk_high(at, g, n, p, which, st, layer):
                made(at, n)
                dst = (qa, ka)[which // 2]
                cols = slice((which % 2) * COLS, (which % 2 + 1) * COLS)
                for h in range(2):
                    last = act.activation(dst[own(h), st, h, cols], g[own(h), :], ACT.Identity,
                                          bias=biases[own(h), layer, (which // 2) * CT + p:(which // 2) * CT + p + 1])
                last.then_inc(g_high.sem, 1)

            def v_high(at, g, n, group, st):
                made(at, n)
                act.activation(v[:, st, 4 * group:4 * group + 4, :, 0:HALF],
                               g[:, :].rearrange("p (m h d) -> p m h d", m=4, h=2), ACT.Copy).then_inc(g_high.sem, 1)

            def turn_high(at, layer, p, half):
                n = ITEMS[layer]["turn", p, half]
                made(at, n)
                act.activation(o_hi[:, p, half * COLS:(half + 1) * COLS], bank_of(layer, n)[:, :], ACT.Identity,
                               bias=biases[:, layer, 2 * CT + p:2 * CT + p + 1]).then_inc(g_high.sem, 1)

            def x_split(at, layer, kt):
                if layer == 0:
                    act.wait_ge(x_loaded.sem, at(x_loaded, 16 * CT))
                else:
                    act.wait_ge(x_normed.sem, at(x_normed, kt + 1))
                act.activation(x_hi[:, kt, :], x_in[:, kt, :], ACT.Copy).then_inc(x_high.sem, 1)

            act.wait_ge(const_ready, 1)
            act.wait_ge(params_ready, 1)
            for layer in range(2):
                at = lead_at(layer)
                if layer == 1:
                    act.wait_ge(g_made.sem, at(g_made, 0))
                for kt in range(CT):
                    act.wait_ge(w_loaded[kt].sem, at(w_loaded[kt], 32))
                    act.activation(w_hi[:, kt, :], w_in[:, kt % 2, :], ACT.Copy, scale=WEIGHT_SCALE).then_inc(w_high.sem, 1)
                for kt in range(CT):
                    x_split(at, layer, kt)
                for which in range(4):
                    qk_high(at, bank_of(layer, which, True), which, 0, which, 0, layer)
                for group in range(2):
                    v_high(at, bank_of(layer, 4 + group, True), 4 + group, group, 0)

                with act.Fori(0, NB) as i:
                    at = batch_at(layer, i)
                    for T in range(BSLOTS):
                        p, t = T // SLOTS, T % SLOTS
                        st1, p1 = (p + 1) % 2, (p + 1) % PAIRS
                        u = T // MT
                        if t in QK_EVICT:
                            n = ITEMS[layer]["qk", p, QK_EVICT[t]]
                            qk_high(at, bank_of(layer, n), n, p1, QK_EVICT[t], st1, layer)
                        if t in TURN_EVICT and p:
                            turn_high(at, layer, p - 1, TURN_EVICT[t])
                        if t in V_EVICT:
                            n = ITEMS[layer]["v", p, V_EVICT[t]]
                            v_high(at, bank_of(layer, n), n, V_EVICT[t], st1)
                        if p == NEXT_X_PAIR and t >= NEXT_X_SLOT:
                            x_split(at, layer, t - NEXT_X_SLOT)
                        act.wait_ge(s_made.sem, at(s_made, T + 1))
                        if T % MT == 0 and u >= 2:
                            act.wait_ge(o_made.sem, at(o_made, u - 1))
                        if T % 2 == 0 and T >= 4:
                            act.wait_ge(p_rest.sem, at(p_rest, T // 2 - 1))
                        s = s_bank[T % 2]
                        act.activation(p_f32[:, (T // 2) % 2, T % 2, :], s[:, :], ACT.Exp, scale=EXP_SCALE)
                        act.activation(p_hi[:, u % 2, T % MT, :], s[:, :], ACT.Exp, scale=EXP_SCALE).then_inc(p_made.sem, 1)
                    for half in range(2):
                        turn_high(at, layer, PAIRS - 1, half)
                    act.wait_ge(y_stored.sem, at(y_stored, 0))
                    for ot in range(CT):
                        for nh in range(NH):
                            n = ITEMS[layer]["proj", ot, nh]
                            made(at, n)
                            act.activation(yb[:, ot, nh * COLS:(nh + 1) * COLS], bank_of(layer, n)[:, :], ACT.Identity,
                                           bias=biases[:, layer, 3 * CT + ot:3 * CT + ot + 1],
                                           scale=1.0 / WEIGHT_SCALE ** 2).then_inc(g_high.sem, 1)
                    if layer == 0:
                        act.wait_ge(norm_ready.sem, at(norm_ready, 1))
                        for ot in range(CT):
                            act.activation(yb[:, ot, :], yb[:, ot, :], ACT.Identity, bias=norm_b[:, ot:ot + 1],
                                           scale=norm_a[:, ot:ot + 1]).then_inc(y_scaled.sem, 1)

        @block.vector
        def _(dve):
            def qk_low(at, g, n, n_high, p, which, st, layer):
                dve.wait_ge(g_high.sem, at(g_high, n_high + 1))
                high, low = ((qa, qb), (ka, ka))[which // 2]
                cols = slice((which % 2) * COLS, (which % 2 + 1) * COLS)
                for h in range(2):
                    rows = own(h) if which < 2 else own(1 - h)
                    last = dve.scalar_tensor_tensor(
                        out=low[rows, st, h, cols], in0=g[own(h), :],
                        scalar=biases[own(h), layer, (which // 2) * CT + p:(which // 2) * CT + p + 1],
                        in1=high[own(h), st, h, cols], op0=ALU.add, op1=ALU.subtract)
                last.then_inc(g_free.sem, 1)

            def v_low(at, g, n, n_high, group, st):
                dve.wait_ge(g_high.sem, at(g_high, n_high + 1))
                dve.tensor_tensor(v[:, st, 4 * group:4 * group + 4, :, VL:VL + HALF],
                                  g[:, :].rearrange("p (m h d) -> p m h d", m=4, h=2),
                                  v[:, st, 4 * group:4 * group + 4, :, 0:HALF], ALU.subtract).then_inc(g_free.sem, 1)

            def turn_low(at, layer, p, half):
                n = ITEMS[layer]["turn", p, half]
                dve.wait_ge(g_high.sem, at(g_high, HIGHS[layer]["turn", p, half] + 1))
                cols = slice(half * COLS, (half + 1) * COLS)
                dve.scalar_tensor_tensor(out=o_lo[:, p, cols], in0=bank_of(layer, n)[:, :],
                                         scalar=biases[:, layer, 2 * CT + p:2 * CT + p + 1], in1=o_hi[:, p, cols],
                                         op0=ALU.add, op1=ALU.subtract).then_inc(g_free.sem, 1)

            def read_max(at, n, h, k):
                dve.wait_ge(max_made.sem, at(max_made, n + 1))
                dve.tensor_reduce(maxes[:, h, k:k + 1], m_bank[n % 2][:, :], AX.X, ALU.max).then_inc(max_read.sem, 1)

            def make_shift(at, n_read, n_shift, h):
                dve.wait_ge(max_read.sem, at(max_read, n_read))
                halves = maxes[:, h, :].rearrange("p (a b) -> p a b", b=2)
                dve.tensor_tensor(row_max[:, h, :], halves[:, :, 0], halves[:, :, 1], ALU.max).then_inc(max_joined.sem, 1)
                dve.wait_ge(max_joined.sem, at(max_joined, n_shift + 1))
                dve.tensor_scalar(shift[:, h, :], row_max[:, h, :], -1.0 / SHIFT_UNIT, SHIFT_BONUS, ALU.mult, ALU.add)\
                    .then_inc(shift_ready.sem, 1)

            def copy_shift(at, g, n, h):
                dve.wait_ge(g_made.sem, at(g_made, n + 1))
                dve.tensor_copy(shift_rows[:, h, :], g[0:MT, 0:HALF].bitcast(F16)).then_inc(g_free.sem, 1)

            def exp_rest(at, j):
                u, mt = (2 * j) // MT, (2 * j) % MT
                dve.wait_ge(p_made.sem, at(p_made, 2 * j + 2))
                dve.tensor_tensor(p_lo[:, u % 2, mt:mt + 2, :], p_f32[:, j % 2, :, :], p_hi[:, u % 2, mt:mt + 2, :],
                                  ALU.subtract).then_inc(p_rest.sem, 1)

            def divide(at, layer, u):
                p, h, nh = u // 4, (u // 2) % 2, u % 2
                dve.wait_ge(o_made.sem, at(o_made, u + 1))
                if u % 4 == 0 and p:
                    dve.wait_ge(g_made.sem, at(g_made, ITEMS[layer]["turn", p - 1, 1] + 1))
                o = o_bank[u % 2][:, 0:QT * (HALF + 1)].rearrange("p (q d) -> p q d", d=HALF + 1)
                dve.reciprocal(recip[:, u % 2, :], o[:, :, HALF]).then_inc(o_recip.sem, 1)
                dve.wait_ge(o_recip.sem, at(o_recip, u + 1))
                dve.tensor_tensor(o_pair[:, nh * QT:(nh + 1) * QT, own(h)], o[:, :, 0:HALF],
                                  recip[:, u % 2, :].unsqueeze(2).to_broadcast([P, QT, HALF]), ALU.mult).then_inc(o_read.sem, 1)

            def x_normalise(at, kt, index):
                dve.wait_ge(x_loaded.sem, at(x_loaded, 16 * CT))
                dve.tensor_scalar(x_in[:, kt, :], x_in[:, kt, :], next_a[:, index, kt:kt + 1].rearrange("p b o -> p (b o)"),
                                  next_b[:, index, kt:kt + 1].rearrange("p b o -> p (b o)"), ALU.mult, ALU.add)\
                    .then_inc(x_normed.sem, 1)

            def x_rest(at, kt):
                dve.wait_ge(x_high.sem, at(x_high, kt + 1))
                dve.tensor_tensor(x_lo[:, kt, :], x_in[:, kt, :], x_hi[:, kt, :], ALU.subtract).then_inc(x_low.sem, 1)

            dve.wait_ge(const_ready, 1)
            dve.wait_ge(params_in, 96)
            dve.tensor_scalar(biases[:, 1, 0:3 * CT], biases[:, 1, 0:3 * CT], WEIGHT_SCALE, None, ALU.mult)\
                .then_inc(params_ready, 1)
            dve.wait_ge(params_ready, 1)
            dve.engine_nop().then_inc(res_added.sem, 1)
            dve.engine_nop().then_inc(y_stored.sem, 1)

            for layer in range(2):
                at = lead_at(layer)
                for kt in range(CT):
                    dve.wait_ge(w_high.sem, at(w_high, kt + 1))
                    dve.scalar_tensor_tensor(out=w_lo[:, kt, :], in0=w_in[:, kt % 2, :], scalar=WEIGHT_SCALE,
                                             in1=w_hi[:, kt, :], op0=ALU.mult, op1=ALU.subtract).then_inc(w_low.sem, 1)
                if layer == 1:
                    for kt in range(CT):
                        x_normalise(at, kt, slice(0, 1))
                for kt in range(CT):
                    x_rest(at, kt)
                for which in range(4):
                    qk_low(at, bank_of(layer, which, True), which, which, 0, which, 0, layer)
                for group in range(2):
                    v_low(at, bank_of(layer, 4 + group, True), 4 + group, 4 + group, group, 0)
                for k in range(16):
                    read_max(at, k, 0, k)
                make_shift(at, 16, 0, 0)
                for k in range(4):
                    read_max(at, 16 + k, 1, k)
                copy_shift(at, bank_of(layer, 6, True), 6, 0)

                with dve.Fori(0, NB) as i:
                    at = batch_at(layer, i)
                    following = bass.ds((i + 1) % NB, 1)
                    n_max = 0
                    n_link = [0]

                    def link(ins):
                        n_link[0] += 1
                        ins.then_inc(links.sem, 1)
                        dve.wait_ge(links.sem, at(links, n_link[0]))

                    def norm_factors(which, weight, bias, a_out, b_out):
                        n = ITEMS[layer]["norm", which, 0]
                        dve.memset(tmp[:, :], 0.0)
                        for ot in range(CT):
                            last = dve.bn_aggr(mv[:, ot, :], bn[:, ot, :, :].rearrange("p a s -> p (a s)"))
                        link(last)
                        dve.tensor_copy(gs[:, 0:CT], mv[:, :, 0])
                        link(dve.tensor_tensor(tmp[:, :], mv[:, :, 0], mv[:, :, 0], ALU.mult))
                        dve.tensor_tensor(gs[:, CT:2 * CT], tmp[:, :], mv[:, :, 1], ALU.add).then_inc(stats_ready.sem, 1)
                        dve.wait_ge(g_made.sem, at(g_made, n + 1))
                        dve.tensor_copy(gm[:, :], bank_of(layer, n)[:, 0:2 * CT]).then_inc(g_free.sem, 1)
                        dve.wait_ge(g_free.sem, at(g_free, n + 1))
                        link(dve.tensor_tensor(tmp[:, :], gm[:, 0:CT], gm[:, 0:CT], ALU.mult))
                        link(dve.scalar_tensor_tensor(out=tmp[:, :], in0=gm[:, CT:2 * CT], scalar=1.0, in1=tmp[:, :],
                                                      op0=ALU.mult, op1=ALU.subtract))
                        dve.tensor_scalar(var[:, :], tmp[:, :], EPS, None, ALU.add).then_inc(var_ready.sem, 1)
                        dve.wait_ge(rstd_ready.sem, at(rstd_ready, which + 1))
                        link(dve.tensor_tensor(a_out, rstd[:, :], weight, ALU.mult))
                        link(dve.tensor_tensor(tmp[:, :], gm[:, 0:CT], a_out, ALU.mult))
                        dve.tensor_tensor(b_out, bias, tmp[:, :], ALU.subtract).then_inc(norm_ready.sem, 1)

                    for T in range(BSLOTS):
                        p, t = T // SLOTS, T % SLOTS
                        st1, p1 = (p + 1) % 2, (p + 1) % PAIRS
                        if t == SHIFT_B_CHAIN:
                            make_shift(at, n_max, 2 * p, 1)
                        if t == SHIFT_A_CHAIN:
                            make_shift(at, n_max, 2 * p + 1, 0)
                        for h, ahead, k in max_tiles(t):
                            read_max(at, n_max, h, k)
                            n_max += 1
                        if T % 2 == 0 and T >= 2:
                            exp_rest(at, T // 2 - 1)
                        if T % MT == 0 and T >= 2 * MT:
                            divide(at, layer, T // MT - 2)
                        if t in QK_EVICT:
                            which = QK_EVICT[t]
                            n = ITEMS[layer]["qk", p, which]
                            qk_low(at, bank_of(layer, n), n, HIGHS[layer]["qk", p, which], p1, which, st1, layer)
                        if t in TURN_EVICT and p:
                            turn_low(at, layer, p - 1, TURN_EVICT[t])
                        if t == SHIFT_B_COPY:
                            n = ITEMS[layer]["shift", p, 1]
                            copy_shift(at, bank_of(layer, n), n, 1)
                        if t == SHIFT_A_COPY:
                            n = ITEMS[layer]["shift", p, 0]
                            copy_shift(at, bank_of(layer, n), n, 0)
                        if t in V_EVICT:
                            group = V_EVICT[t]
                            n = ITEMS[layer]["v", p, group]
                            v_low(at, bank_of(layer, n), n, HIGHS[layer]["v", p, group], group, st1)
                        T_x = T - NEXT_X_PAIR * SLOTS - NEXT_X_SLOT
                        if layer == 1 and -1 <= T_x < CT - 1:
                            x_normalise(at, T_x + 1, following)
                        if 1 <= T_x < CT + 1:
                            x_rest(at, T_x - 1)
                    exp_rest(at, BSLOTS // 2 - 1)
                    divide(at, layer, UNITS - 2)
                    divide(at, layer, UNITS - 1)
                    for half in range(2):
                        turn_low(at, layer, PAIRS - 1, half)
                    dve.wait_ge(res_loaded.sem, at(res_loaded, 16 * CT))
                    for ot in range(CT):
                        for nh in range(NH):
                            dve.wait_ge(g_high.sem, at(g_high, HIGHS[layer]["proj", ot, nh] + 1))
                            cols = slice(nh * COLS, (nh + 1) * COLS)
                            if layer == 0:
                                dve.bn_stats(bn[:, ot, nh, :], yb[:, ot, cols]).then_inc(g_free.sem, 1)
                            else:
                                dve.tensor_tensor(yb[:, ot, cols], yb[:, ot, cols], x_res[:, ot, cols], ALU.add)\
                                    .then_inc(res_added.sem, 1)
                                dve.engine_nop().then_inc(g_free.sem, 1)
                    if layer == 0:
                        dve.wait_ge(g_free.sem, at(g_free, ITEMS[layer]["proj", CT - 1, NH - 1] + 1))
                        norm_factors(0, affine[:, 0, :], affine[:, 1, :], norm_a[:, :], norm_b[:, :])
                        for ot in range(CT):
                            dve.wait_ge(y_scaled.sem, at(y_scaled, ot + 1))
                            dve.tensor_tensor(yb[:, ot, :], yb[:, ot, :], x_res[:, ot, :], ALU.add)\
                                .then_inc(res_added.sem, 1)
                            dve.wait_ge(res_added.sem, at(res_added, ot + 1))
                            for nh in range(NH):
                                last = dve.bn_stats(bn[:, ot, nh, :], yb[:, ot, nh * COLS:(nh + 1) * COLS])
                        link(last)
                        here = bass.ds(i, 1)
                        norm_factors(1, affine[:, 2, :], affine[:, 3, :],
                                     next_a[:, here, :].rearrange("p b o -> p (b o)"),
                                     next_b[:, here, :].rearrange("p b o -> p (b o)"))
                        assert n_link[0] == links.per[0], n_link[0]


_INS = ["x", "L0_conv_w_qkv", "L0_conv_w_proj", "L0_conv_gamma", "L0_conv_beta", "L1_conv_norm_w", "L1_conv_norm_b",
        "L1_conv_qkv_w", "L1_conv_qkv_b", "L1_conv_proj_w", "L1_conv_proj_b"]
_TURNED = {"L0_conv_w_qkv", "L0_conv_w_proj", "L1_conv_qkv_w", "L1_conv_proj_w"}


def kernel(**inputs):
    import numpy as _np
    import concourse.bacc as _bacc
    from concourse import mybir as _mybir
    from concourse.bass_utils import run_bass_kernel_spmd as _run

    nc = _bacc.Bacc("TRN2", target_bir_lowering=False, num_devices=1)
    arrays, args = {}, []
    for name in _INS:
        a = _np.asarray(inputs[name])
        if name == "x":
            b, c, h, w = a.shape
            a = a.reshape(b, c, h * w)
        if name in _TURNED:
            a = a.T
        if a.ndim == 1:
            a = a.reshape(-1, 128).T
        a = _np.ascontiguousarray(a)
        arrays[f"in_{name}_dram"] = a
        args.append(nc.dram_tensor(f"in_{name}_dram", a.shape, _mybir.dt.from_np(a.dtype), kind="ExternalInput").ap())
    args.append(nc.dram_tensor("out_0_dram", (b, c, h * w), _mybir.dt.float32, kind="ExternalOutput").ap())
    two_attention_blocks(nc, *args)
    r = _run(nc, [arrays], core_ids=[0])
    return _np.asarray(r.results[0]["out_0_dram"]).reshape(b, c, h, w)
```

```python
import math
from contextlib import ExitStack

import concourse.bass as bass
from concourse import mybir

F32 = mybir.dt.float32
F16 = mybir.dt.float16
ALU = mybir.AluOpType
ACT = mybir.ActivationFunctionType
AX = mybir.AxisListType

P = 128
HALF = 64
COLS = 512
EPS = 1e-5
WEIGHT_SCALE = 16.0
SHIFT_UNIT = 1024.0
HEADROOM = 256.0


class Tally:

    def __init__(self, sem, lead, first, per, tail, batches):
        self.sem, self.lead, self.first, self.per, self.tail = sem, lead, first, per, tail
        self.batches = batches
        self.start = [0]
        for n in range(len(per)):
            self.start.append(self.start[-1] + lead[n] + first[n] + (batches - 1) * per[n] + tail[n])

    def value(self, layer, when, n):
        base = self.start[layer]
        if isinstance(when, str) and when == "lead":
            return base + n
        base += self.lead[layer] + n
        if isinstance(when, str) and when == "tail":
            return base + self.first[layer] + (self.batches - 1) * self.per[layer]
        if isinstance(when, int) and when == 0:
            return base
        return base + self.first[layer] - self.per[layer] + when * self.per[layer]


SLOTS = 32
QK_SLOTS = range(1, 13)
TURN_SLOTS = {12: 0, 15: 1}
NORM_SLOT = 14
QUEUE_FIRST = (16, 16, 16, 16)
V_LAST = (29, 29, 22, 29)
PROJ_LAST = 30
MAX_B_SLOTS, SHIFT_B_CHAIN = 12, 12
MAX_A_FIRST, SHIFT_A_CHAIN = 13, 27
PV_OFFSETS = {2: 0, 4: 1, 5: 2, 7: 3}
NEXT_X_PAIR, NEXT_X_SLOTS = 2, {23: 0, 25: 1, 27: 2, 29: 3}
NORMALISE_SLOTS = {8: 0, 10: 1, 12: 2, 14: 3}
STATS_SLOT, VAR_SLOT, FACTOR_SLOT = 2, 15, 18
APPLY_SLOTS = {19: 0, 22: 1, 25: 2, 28: 3}
GPSIMD_SHARE = (0, 1, 2, 3)


def max_order():
    tiles = [[(h, k) for k in range(16)] for h in range(2)]
    return tiles[1] + [(1, None)] + tiles[0] + [(0, None)]


def max_slots():
    found = {t: [] for t in range(SLOTS)}
    for n in range(16):
        found[n * MAX_B_SLOTS // 16].append(n)
    found[SHIFT_B_CHAIN + 1].append(16)
    for n in range(16):
        found[MAX_A_FIRST + n * (SHIFT_A_CHAIN - MAX_A_FIRST) // 16].append(17 + n)
    found[SHIFT_A_CHAIN + 1].append(33)
    return found


def spread(costs, first, last):
    total, done, n, out = sum(costs), 0.0, 0, {}
    for t in range(first, last + 1):
        k = n
        while n < len(costs) and done < total * (t + 1 - first) / (last + 1 - first) - 1e-9:
            done += costs[n]
            n += 1
        out[t] = (k, n)
    assert n == len(costs)
    return out


def two_attention_blocks(
    nc: bass.Bass,
    x, w_qkv0, w_proj0, gamma0, beta0, norm_w1, norm_b1, w_qkv1, qkv_b1, w_proj1, proj_b1,
    out,
):
    NB, C, N = x.shape
    CT = C // P
    PAIRS = C // P
    HEADS = 2 * PAIRS
    MT = N // P
    NH = N // COLS
    QT = COLS // P
    WCOLS = 4 * C
    BSLOTS = PAIRS * SLOTS
    UNITS = 2 * NH * PAIRS
    RING = 4
    GROUP = 64
    EXP_SCALE = float(HALF) ** -0.5 / WEIGHT_SCALE ** 2
    VW = 136
    VL = 72
    SHIFT_BONUS = math.log(HEADROOM) / EXP_SCALE / SHIFT_UNIT
    assert (CT, PAIRS, MT, NH, 2 * NH * MT) == (4, 4, 8, 2, SLOTS)

    MAX_ORDER, MAX_SLOTS = max_order(), max_slots()
    N_MAX = len(MAX_ORDER)
    N_B = N_MAX // 2

    def step_items(layer, first, p):
        items = [("qk", p, k) for k in range(4)]
        if p or not first:
            items += [("turn", (p - 1) % PAIRS, 0)]
        if layer == 0 and not first and p in (1, 2):
            items += [("norm", p - 1, 0)]
        if p or not first:
            items += [("turn", (p - 1) % PAIRS, 1)]
        items += [("v", p, 0), ("v", p, 1)]
        if p == 0 and not first:
            items += [("proj", ot, nh) for ot in range(CT) for nh in range(NH)]
        return items

    def items_of(layer, when):
        if isinstance(when, str) and when == "lead":
            return [("qk", -1, k) for k in range(4)] + [("v", -1, 0), ("v", -1, 1)]
        if isinstance(when, str) and when == "tail":
            return [("turn", PAIRS - 1, 0), ("turn", PAIRS - 1, 1)] + \
                [("proj", ot, nh) for ot in range(CT) for nh in range(NH)] + \
                ([("norm", 0, 0), ("norm", 1, 0)] if layer == 0 else [])
        first = isinstance(when, int) and when == 0
        return [it for p in range(PAIRS) for it in step_items(layer, first, p)]

    KINDS = ("lead", 0, 1, "tail")
    ORDER = [{k: items_of(layer, k) for k in KINDS} for layer in range(2)]
    INDEX = [{k: {it: n for n, it in enumerate(ORDER[layer][k])} for k in KINDS} for layer in range(2)]
    HIGHS = [{k: {it: n for n, it in enumerate(i for i in ORDER[layer][k] if i[0] != "norm")} for k in KINDS}
             for layer in range(2)]
    assert all(len(ORDER[layer][k]) % 2 == 0 for layer in range(2) for k in KINDS)

    def kind(when):
        return when if isinstance(when, str) else (0 if isinstance(when, int) and when == 0 else 1)

    def index(layer, when, item):
        return INDEX[layer][kind(when)][item]

    def high_index(layer, when, item):
        return HIGHS[layer][kind(when)][item]

    def queue_slots(first, p):
        items = [("v", p, 0), ("v", p, 1)]
        last = V_LAST[p]
        if p == 0 and not first:
            items += [("proj", ot, nh) for ot in range(CT) for nh in range(NH)]
            last = PROJ_LAST
        flat = [(it, k) for it in items for k in range(4 * 3 * CT if it[0] == "v" else 3 * CT)]
        found = {}
        for t, (k0, k1) in spread([1.0 if it[0] == "v" else 4.0 for it, _ in flat], QUEUE_FIRST[p], last).items():
            parts = {}
            for it, k in flat[k0:k1]:
                parts.setdefault(it, []).append(k)
            found[t] = [(it, ks[0], ks[-1] + 1) for it, ks in parts.items()]
        return found

    def evictions(first, p):
        found = {t: [] for t in range(SLOTS)}
        for k in range(4):
            found[QK_SLOTS[3 * k + 2] + 1].append(("qk", p, k))
        if p or not first:
            for t, half in TURN_SLOTS.items():
                found[t + 1].append(("turn", (p - 1) % PAIRS, half))
        for t, parts in queue_slots(first, p).items():
            for it, _, k1 in parts:
                if k1 == (4 * 3 * CT if it[0] == "v" else 3 * CT):
                    found[t + 1].append(it)
        return found

    with ExitStack() as ctx:
        def sb(name, shape, dt):
            return ctx.enter_context(nc.sbuf_tensor(name, shape, dt))

        def bank(name):
            return ctx.enter_context(nc.psum_tensor(name, [P, COLS], F32))

        def both(n):
            return list(n) if isinstance(n, (list, tuple)) else [n, n]

        def tally(name, lead, per, first=None, tail=0):
            return Tally(ctx.enter_context(nc.semaphore(name)), both(lead), both(per if first is None else first),
                         both(per), both(tail), NB)

        y_dram = nc.dram_tensor("y_scratch", (NB, C, N), F32, kind="Internal").ap()

        w_hi = sb("w_hi", [P, CT, WCOLS], F16)
        w_lo = sb("w_lo", [P, CT, WCOLS], F16)
        x_in = sb("x_in", [P, CT, N], F32)
        x_res = sb("x_res", [P, CT, N], F32)
        x_hi = sb("x_hi", [P, CT, N], F16)
        x_lo = sb("x_lo", [P, CT, N], F16)
        qa = sb("qa", [P, 2, 2, N], F16)
        qb = sb("qb", [P, 2, 2, N], F16)
        ka = sb("ka", [P, 2, 2, N], F16)
        kb = sb("kb", [P, 2, 2, N], F16)
        v = sb("v", [P, 2, MT, 2, VW], F16)
        p_f32 = sb("p_f32", [P, RING, 2, COLS], F32)
        p_hi = sb("p_hi", [P, 2, MT, COLS], F16)
        p_lo = sb("p_lo", [P, 2, MT, COLS], F16)
        o_pair = sb("o_pair", [P, MT, P], F32)
        o_hi = sb("o_hi", [P, CT, N], F16)
        o_lo = sb("o_lo", [P, CT, N], F16)
        yb = sb("yb", [P, CT, N], F32)
        w_in = yb[:, :, :].rearrange("p (a b) n -> p a (b n)", a=2)
        ident = sb("ident", [P, P], F32)
        ident16 = sb("ident16", [P, P], F16)
        group_mean = sb("group_mean", [P, P], F32)
        biases = sb("biases", [P, 2, 4 * CT], F32)
        affine = sb("affine", [P, 4, CT], F32)
        maxes = sb("maxes", [P, 2, 2 * MT], F32)
        row_max = sb("row_max", [P, 2, MT], F32)
        shift = sb("shift", [P, 2, MT], F16)
        shift_rows = sb("shift_rows", [MT, 2, P], F16)
        recip = sb("recip", [P, 2, QT], F32)
        bn = sb("bn", [P, CT, NH, 6], F32)
        mv = sb("mv", [P, CT, 2], F32)
        gs = sb("gs", [P, 2 * CT], F32)
        gm = sb("gm", [P, 2 * CT], F32)
        var = sb("var", [P, CT], F32)
        rstd = sb("rstd", [P, CT], F32)
        tmp = sb("tmp", [P, CT], F32)
        minus_half = sb("minus_half", [P, CT], F32)
        norm_a = sb("norm_a", [P, CT], F32)
        norm_b = sb("norm_b", [P, CT], F32)
        next_a = sb("next_a", [P, NB, CT], F32)
        next_b = sb("next_b", [P, NB, CT], F32)

        s_bank = [bank("s_bank0"), bank("s_bank1")]
        m_bank = [bank("m_bank0"), bank("m_bank1")]
        o_bank = [bank("o_bank0"), bank("o_bank1")]
        g_bank = [bank("g_bank0"), bank("g_bank1")]

        const_ready = ctx.enter_context(nc.semaphore("const_ready"))
        const_step = ctx.enter_context(nc.semaphore("const_step"))
        params_in = ctx.enter_context(nc.semaphore("params_in"))
        params_ready = ctx.enter_context(nc.semaphore("params_ready"))

        def lens(table, k):
            return [len(table[layer][k]) for layer in range(2)]

        w_loaded = [tally(f"w_loaded{k}", 32, 0) for k in range(CT)]
        w_high = tally("w_high", CT, 0)
        w_low = tally("w_low", CT, 0)
        x_loaded = tally("x_loaded", 16 * CT, 16 * CT)
        x_normed = tally("x_normed", (0, CT), (0, CT))
        x_high = tally("x_high", CT, CT)
        x_low = tally("x_low", CT, CT)
        g_made = tally("g_made", lens(ORDER, "lead"), lens(ORDER, 1), lens(ORDER, 0), lens(ORDER, "tail"))
        g_free = tally("g_free", lens(ORDER, "lead"), lens(ORDER, 1), lens(ORDER, 0), lens(ORDER, "tail"))
        g_high = tally("g_high", lens(HIGHS, "lead"), lens(HIGHS, 1), lens(HIGHS, 0), lens(HIGHS, "tail"))
        q_copied = tally("q_copied", 32, 32 * PAIRS)
        k_copied = tally("k_copied", 32, 32 * PAIRS)
        max_made = tally("max_made", N_MAX - N_B, PAIRS * N_MAX)
        max_read = tally("max_read", N_MAX - N_B, PAIRS * N_MAX)
        max_joined = tally("max_joined", 1, HEADS)
        shift_ready = tally("shift_ready", 1, HEADS)
        shift_placed = [tally("shift_placed0", 16, 16 * PAIRS), tally("shift_placed1", 0, 16 * PAIRS)]
        s_made = tally("s_made", 0, BSLOTS)
        p_made = tally("p_made", 0, BSLOTS)
        SHARE_V = [k for k in range(MT // 2) if k not in GPSIMD_SHARE]
        rest_v = tally("rest_v", 0, UNITS * len(SHARE_V))
        rest_g = tally("rest_g", 0, UNITS * len(GPSIMD_SHARE))
        o_made = tally("o_made", 0, UNITS)
        o_recip = tally("o_recip", 0, UNITS)
        o_read = tally("o_read", 0, UNITS)
        res_loaded = tally("res_loaded", 0, 16 * CT)
        ADDS = [CT, CT * NH]
        res_added = tally("res_added", 0, ADDS, 0, ADDS)
        y_scaled = tally("y_scaled", 0, [CT, 0], 0, [CT, 0])
        y_stored = tally("y_stored", (1, 0), 16 * CT, 0, 16 * CT)
        stats_ready = tally("stats_ready", 0, [2, 0], 0, [2, 0])
        var_ready = tally("var_ready", 0, [2, 0], 0, [2, 0])
        rstd_ready = tally("rstd_ready", 0, [2, 0], 0, [2, 0])
        norm_ready = tally("norm_ready", 0, [2, 0], 0, [2, 0])
        links = tally("links", 0, [13, 0], 0, [13, 0])

        block = ctx.enter_context(nc.Block())

        def own(h):
            return slice(h * HALF, (h + 1) * HALF)

        def other_row(h):
            return HALF if h == 0 else 0

        def at(t, layer, when, n):
            return t.value(layer, when, n)

        def bank_of(layer, when, item):
            return g_bank[index(layer, when, item) % 2]

        def shifts_until(n0, h):
            return 1 if n0 < 0 else 2 * (n0 // N_MAX) + 2 - h

        def rest_wait(eng, layer, when, j):
            u, k = j // (MT // 2), j % (MT // 2)
            if k in GPSIMD_SHARE:
                eng.wait_ge(rest_g.sem, at(rest_g, layer, when, u * len(GPSIMD_SHARE) + GPSIMD_SHARE.index(k) + 1))
            else:
                eng.wait_ge(rest_v.sem, at(rest_v, layer, when, u * len(SHARE_V) + SHARE_V.index(k) + 1))

        def rest_of_exp(eng, layer, when, j, tally_of):
            u, mt = (2 * j) // MT, (2 * j) % MT
            eng.wait_ge(p_made.sem, at(p_made, layer, when, 2 * j + 2))
            eng.tensor_tensor(p_lo[:, u % 2, mt:mt + 2, :], p_f32[:, j % RING, :, :], p_hi[:, u % 2, mt:mt + 2, :],
                              ALU.subtract).then_inc(tally_of.sem, 1)

        @block.sync
        def _(sp):
            def copy_q(layer, when, p, st):
                sp.wait_ge(g_high.sem, at(g_high, layer, when, high_index(layer, when, ("qk", p, 1)) + 1))
                for h in range(2):
                    sp.dma_start(qa[own(1 - h), st, h, :], qa[own(h), st, h, :]).then_inc(q_copied.sem, 16)

            def copy_k(layer, when, p, st):
                sp.wait_ge(g_high.sem, at(g_high, layer, when, high_index(layer, when, ("qk", p, 3)) + 1))
                for h in range(2):
                    sp.dma_start(kb[own(h), st, h, :], ka[own(h), st, h, :]).then_inc(k_copied.sem, 16)

            def place_shift(layer, when, n, st, h):
                sp.wait_ge(max_read.sem, at(max_read, layer, when, n))
                r = other_row(h)
                sp.dma_start(qb[r:r + 1, st, h, :].rearrange("o (a n) -> o a n", a=MT), shift_rows[:, h, :])\
                    .then_inc(shift_placed[h].sem, 16)

            def load_x(source, which):
                for kt in range(CT):
                    sp.dma_start(x_in[:, kt, :], source[which, kt * P:(kt + 1) * P, :].rearrange("b p n -> p (b n)"))\
                        .then_inc(x_loaded.sem, 16)

            def store_y(layer, when, target, which):
                for ot in range(CT):
                    sp.wait_ge(res_added.sem, at(res_added, layer, when, (ot + 1) * ADDS[layer] // CT))
                    sp.dma_start(target[which, ot * P:(ot + 1) * P, :].rearrange("b p n -> p (b n)"), yb[:, ot, :])\
                        .then_inc(y_stored.sem, 16)

            def batch(layer, b, here, before, following, source, target):
                first = kind(b) == 0
                sp.wait_ge(x_low.sem, at(x_low, layer, b, 0))
                load_x(source, following)
                for p in range(PAIRS):
                    st = (p + 1) % 2
                    copy_q(layer, b, p, st)
                    place_shift(layer, b, p * N_MAX + N_B, p % 2, 1)
                    copy_k(layer, b, p, st)
                    if p == (2, 1)[layer] and not first:
                        store_y(layer, b, target, before)
                    if p == PAIRS - 1:
                        if layer or not first:
                            sp.wait_ge(res_added.sem, at(res_added, layer, b, 0 if first else ADDS[layer]))
                        for ot in range(CT):
                            sp.dma_start(x_res[:, ot, :],
                                         source[here, ot * P:(ot + 1) * P, :].rearrange("b p n -> p (b n)"))\
                                .then_inc(res_loaded.sem, 16)
                    place_shift(layer, b, (p + 1) * N_MAX, st, 0)

            sp.dma_start(biases[:, 1, 0:3 * CT], qkv_b1).then_inc(params_in, 16)
            sp.dma_start(biases[:, 1, 3 * CT:4 * CT], proj_b1).then_inc(params_in, 16)
            for n, a in enumerate((gamma0, beta0, norm_w1, norm_b1)):
                sp.dma_start(affine[:, n, :], a).then_inc(params_in, 16)
            for layer in range(2):
                wq, wp = ((w_qkv0, w_proj0), (w_qkv1, w_proj1))[layer]
                source = (x, y_dram)[layer]
                target = (y_dram, out)[layer]
                if layer == 1:
                    sp.wait_ge(y_stored.sem, at(y_stored, layer, "lead", 0))
                    sp.wait_ge(norm_ready.sem, at(norm_ready, layer, "lead", 0))
                    sp.wait_ge(x_low.sem, at(x_low, layer, "lead", 0))
                for kt in range(CT):
                    if kt >= 2:
                        sp.wait_ge(w_low.sem, at(w_low, layer, "lead", kt - 1))
                    sp.dma_start(w_in[:, kt % 2, 0:3 * C], wq[kt * P:(kt + 1) * P, :]).then_inc(w_loaded[kt].sem, 16)
                    sp.dma_start(w_in[:, kt % 2, 3 * C:4 * C], wp[kt * P:(kt + 1) * P, :]).then_inc(w_loaded[kt].sem, 16)
                    if kt == 1:
                        load_x(source, slice(0, 1))
                copy_q(layer, "lead", -1, 0)
                copy_k(layer, "lead", -1, 0)
                place_shift(layer, "lead", N_MAX - N_B, 0, 0)
                batch(layer, 0, slice(0, 1), None, slice(1, 2), source, target)
                with sp.Fori(1, NB) as b:
                    batch(layer, b, bass.ds(b, 1), bass.ds(b - 1, 1), bass.ds((b + 1) % NB, 1), source, target)
                store_y(layer, "tail", target, slice(NB - 1, NB))
            sp.wait_ge(y_stored.sem, y_stored.start[2])
            for t in (q_copied, k_copied, *shift_placed):
                sp.wait_ge(t.sem, t.start[2])

        @block.gpsimd
        def _(pool):
            steps = [0]

            def step(ins):
                steps[0] += 1
                ins.then_inc(const_step, 1)
                pool.wait_ge(const_step, steps[0])

            for m in (ident, ident16):
                step(pool.memset(m[:, :], 0.0))
                step(pool.affine_select(out=m[:, :], in_=m[:, :], compare_op=ALU.not_equal, fill=1.0, base=0,
                                        pattern=[[-1, P]], channel_multiplier=1))
            step(pool.memset(group_mean[:, :], 0.0))
            for g in range(P // GROUP):
                step(pool.memset(group_mean[g * GROUP:(g + 1) * GROUP, g * GROUP:(g + 1) * GROUP], 1.0 / GROUP))
            for h in range(2):
                r = other_row(h)
                step(pool.memset(kb[own(1 - h), :, h, :], 0.0))
                step(pool.memset(kb[r:r + 1, :, h, :], SHIFT_UNIT))
                step(pool.memset(qb[own(1 - h), :, h, :], 0.0))
            for st in range(2):
                step(pool.memset(v[:, st, :, :, HALF:HALF + 1], 1.0))
            step(pool.memset(biases[:, 0, :], 0.0))
            pool.memset(minus_half[:, :], -0.5).then_inc(const_ready, 1)
            pool.wait_ge(const_ready, 1)

            def power(layer, when, which):
                pool.wait_ge(var_ready.sem, at(var_ready, layer, when, which + 1))
                pool.tensor_tensor(rstd[:, :], var[:, :], minus_half[:, :], ALU.pow).then_inc(rstd_ready.sem, 1)

            def batch(layer, b):
                for j in range(BSLOTS // 2):
                    if layer == 0 and kind(b) and j in (1 * SLOTS // 2 + 8, 2 * SLOTS // 2 + 8):
                        power(layer, b, j // (SLOTS // 2) - 1)
                    if j % (MT // 2) in GPSIMD_SHARE:
                        rest_of_exp(pool, layer, b, j, rest_g)

            for layer in range(2):
                batch(layer, 0)
                with pool.Fori(1, NB) as b:
                    batch(layer, b)
                if layer == 0:
                    for which in range(2):
                        power(layer, "tail", which)

        @block.tensor
        def _(pe):
            def claim(layer, when, item):
                n = index(layer, when, item)
                if layer or kind(when) != "lead" or n >= 2:
                    pe.wait_ge(g_free.sem, at(g_free, layer, when, n - 1))

            def qk_terms(p, which):
                w0 = (which // 2) * C + p * P
                cols = slice((which % 2) * COLS, (which % 2 + 1) * COLS)
                terms = []
                for kt in range(CT):
                    wh, wl = w_hi[:, kt, w0:w0 + P], w_lo[:, kt, w0:w0 + P]
                    terms += [(wh, x_hi[:, kt, cols]), (wh, x_lo[:, kt, cols]), (wl, x_hi[:, kt, cols])]
                return terms

            def v_terms(p, mt):
                w0 = 2 * C + p * P
                rows = slice(mt * P, (mt + 1) * P)
                terms = []
                for kt in range(CT):
                    wh, wl = w_hi[:, kt, w0:w0 + P], w_lo[:, kt, w0:w0 + P]
                    terms += [(x_hi[:, kt, rows], wh), (x_hi[:, kt, rows], wl), (x_lo[:, kt, rows], wh)]
                return terms

            def proj_terms(ot, nh):
                w0 = 3 * C + ot * P
                cols = slice(nh * COLS, (nh + 1) * COLS)
                terms = []
                for ct in range(CT):
                    wh, wl = w_hi[:, ct, w0:w0 + P], w_lo[:, ct, w0:w0 + P]
                    terms += [(wh, o_hi[:, ct, cols]), (wh, o_lo[:, ct, cols]), (wl, o_hi[:, ct, cols])]
                return terms

            def products(layer, when, item, k0=0, k1=None, p1=0):
                what, a, n = item
                g = bank_of(layer, when, item)
                if what == "v":
                    terms = [t for j in range(4) for t in v_terms(p1, 4 * n + j)]
                    areas = [g[:, j * P:(j + 1) * P] for j in range(4)]
                else:
                    terms = qk_terms(p1, n) if what == "qk" else proj_terms(a, n)
                    areas = [g[:, :]]
                run = len(terms) // len(areas)
                k1 = len(terms) if k1 is None else k1
                if k0 == 0:
                    claim(layer, when, item)
                for k in range(k0, k1):
                    last = pe.matmul(areas[k // run], *terms[k], start=(k % run == 0), stop=(k % run == run - 1))
                if k1 == len(terms):
                    last.then_inc(g_made.sem, 1)

            def max_use(layer, when, n0, n, st):
                h, k = MAX_ORDER[n]
                if layer or kind(when) != "lead" or n >= N_B + 2:
                    pe.wait_ge(max_read.sem, at(max_read, layer, when, n0 + n - 1))
                m = m_bank[n % 2]
                if k is None:
                    pe.wait_ge(shift_ready.sem, at(shift_ready, layer, when, shifts_until(n0, h)))
                    pe.transpose(m[0:MT, 0:HALF].bitcast(F16), shift[:, h, :], ident16[:, :]).then_inc(max_made.sem, 1)
                else:
                    nt, mh = k % MT, k // MT
                    pe.matmul(m[:, :], qa[:, st, h, nt * P:(nt + 1) * P], ka[:, st, h, mh * COLS:(mh + 1) * COLS],
                              start=True, stop=True).then_inc(max_made.sem, 1)

            def turn_output(layer, when, p, half):
                item = ("turn", p, half)
                claim(layer, when, item)
                pe.wait_ge(o_read.sem, at(o_read, layer, when, 0 if p == PAIRS - 1 else 4 * (p + 1)))
                g = bank_of(layer, when, item)
                for j in range(QT):
                    last = pe.transpose(g[:, j * P:(j + 1) * P], o_pair[:, half * QT + j, :], ident[:, :])
                last.then_inc(g_made.sem, 1)

            def average(layer, when, which):
                claim(layer, when, ("norm", which, 0))
                pe.wait_ge(stats_ready.sem, at(stats_ready, layer, when, which + 1))
                pe.matmul(bank_of(layer, when, ("norm", which, 0))[:, 0:2 * CT], group_mean[:, :], gs[:, :],
                          start=True, stop=True).then_inc(g_made.sem, 1)

            def scores(layer, b, T):
                p, h, nh, mt = T // SLOTS, (T % SLOTS) // (NH * MT), (T // MT) % NH, T % MT
                st = p % 2
                s = s_bank[T % 2]
                if layer or kind(b) != 0 or T >= 2:
                    pe.wait_ge(p_made.sem, at(p_made, layer, b, T - 1))
                if T % (NH * MT) == 0:
                    pe.wait_ge(shift_placed[h].sem, at(shift_placed[h], layer, b, 16 * (p + h)))
                if T % SLOTS == 0:
                    pe.wait_ge(k_copied.sem, at(k_copied, layer, b, 32 * p))
                keys, queries = slice(mt * P, (mt + 1) * P), slice(nh * COLS, (nh + 1) * COLS)
                pe.matmul(s[:, :], ka[:, st, h, keys], qa[:, st, h, queries], start=True, stop=False)
                pe.matmul(s[:, :], kb[:, st, h, keys], qb[:, st, h, queries], start=False, stop=True)\
                    .then_inc(s_made.sem, 1)

            def weighted_sum(layer, when, u, k):
                h, st, buf = (u // 2) % 2, (u // 4) % 2, u % 2
                o = o_bank[buf]
                if k == 0:
                    for j in range(MT // 2):
                        if j == MT // 2 - 1 or (j == max(GPSIMD_SHARE, default=-1)):
                            rest_wait(pe, layer, when, (MT // 2) * u + j)
                    if layer or kind(when) != 0 or u >= 2:
                        pe.wait_ge(o_read.sem, at(o_read, layer, when, u - 1))
                    if u % 4 == 0:
                        pe.wait_ge(g_free.sem, at(g_free, layer, when, index(layer, when, ("v", u // 4 - 1, 1)) + 1 if u else 0))
                for mt in range(MT):
                    hi = p_hi[:, buf, mt, k * P:(k + 1) * P]
                    lo = p_lo[:, buf, mt, k * P:(k + 1) * P]
                    c = k * (HALF + 1)
                    pe.matmul(o[:, c:c + HALF + 1], hi, v[:, st, mt, h, 0:HALF + 1], start=(mt == 0), stop=False)
                    pe.matmul(o[:, c:c + HALF], hi, v[:, st, mt, h, VL:VL + HALF], start=False, stop=False)
                    last = pe.matmul(o[:, c:c + HALF + 1], lo, v[:, st, mt, h, 0:HALF + 1], start=False,
                                     stop=(mt == MT - 1))
                if k == QT - 1:
                    last.then_inc(o_made.sem, 1)

            def batch(layer, b):
                first = kind(b) == 0
                for p in range(PAIRS):
                    st1, p1 = (p + 1) % 2, (p + 1) % PAIRS
                    queue = queue_slots(first, p)
                    for t in range(SLOTS):
                        T = p * SLOTS + t
                        scores(layer, b, T)
                        for n in MAX_SLOTS[t]:
                            if n == N_B:
                                pe.wait_ge(q_copied.sem, at(q_copied, layer, b, 32 * (p + 1)))
                            if n in (N_B, N_B + MT):
                                item = ("qk", p, 2 + (n - N_B) // MT)
                                pe.wait_ge(g_free.sem, at(g_free, layer, b, index(layer, b, item) + 1))
                            max_use(layer, b, p * N_MAX, n, p % 2 if n < N_B else st1)
                        if t in QK_SLOTS:
                            if p == PAIRS - 1 and t == QK_SLOTS[0]:
                                pe.wait_ge(x_low.sem, at(x_low, layer, b, CT))
                            n = t - QK_SLOTS[0]
                            products(layer, b, ("qk", p, n // 3), 4 * (n % 3), 4 * (n % 3) + 4, p1)
                        if t in TURN_SLOTS and (p or not first):
                            turn_output(layer, b, (p - 1) % PAIRS, TURN_SLOTS[t])
                        if t == NORM_SLOT and layer == 0 and not first and p in (1, 2):
                            average(layer, b, p - 1)
                        for item, k0, k1 in queue.get(t, []):
                            products(layer, b, item, k0, k1, p1)
                        u = T // MT - 1
                        if T % MT in PV_OFFSETS and (u >= 0 or not first):
                            weighted_sum(layer, b, u, PV_OFFSETS[T % MT])

            pe.wait_ge(const_ready, 1)
            for layer in range(2):
                pe.wait_ge(w_low.sem, at(w_low, layer, "lead", CT))
                pe.wait_ge(x_low.sem, at(x_low, layer, "lead", CT))
                for item in ORDER[layer]["lead"]:
                    products(layer, "lead", item)
                pe.wait_ge(q_copied.sem, at(q_copied, layer, "lead", 32))
                pe.wait_ge(g_free.sem, at(g_free, layer, "lead", index(layer, "lead", ("qk", -1, 3)) + 1))
                for n in range(N_B, N_MAX):
                    max_use(layer, "lead", -N_B, n, 0)
                batch(layer, 0)
                with pe.Fori(1, NB) as b:
                    batch(layer, b)
                for k in range(QT):
                    weighted_sum(layer, "tail", -1, k)
                for half in range(2):
                    turn_output(layer, "tail", PAIRS - 1, half)
                pe.wait_ge(g_free.sem, at(g_free, layer, "tail", index(layer, "tail", ("turn", PAIRS - 1, 1)) + 1))
                for ot in range(CT):
                    for nh in range(NH):
                        products(layer, "tail", ("proj", ot, nh))
                if layer == 0:
                    for which in range(2):
                        average(layer, "tail", which)

        @block.scalar
        def _(act):
            def high(layer, when, item, p1, st):
                what, a, n = item
                act.wait_ge(g_made.sem, at(g_made, layer, when, index(layer, when, item) + 1))
                g = bank_of(layer, when, item)
                cols = slice((n % 2) * COLS, (n % 2 + 1) * COLS)
                if what == "qk":
                    c = (n // 2) * CT + p1
                    for h in range(2):
                        last = act.activation((qa, ka)[n // 2][own(h), st, h, cols], g[own(h), :], ACT.Identity,
                                              bias=biases[own(h), layer, c:c + 1])
                elif what == "v":
                    last = act.activation(v[:, st, 4 * n:4 * n + 4, :, 0:HALF],
                                          g[:, :].rearrange("p (m h d) -> p m h d", m=4, h=2), ACT.Copy)
                elif what == "turn":
                    last = act.activation(o_hi[:, a, cols], g[:, :], ACT.Identity,
                                          bias=biases[:, layer, 2 * CT + a:2 * CT + a + 1])
                else:
                    last = act.activation(yb[:, a, cols], g[:, :], ACT.Identity,
                                          bias=biases[:, layer, 3 * CT + a:3 * CT + a + 1],
                                          scale=1.0 / WEIGHT_SCALE ** 2)
                last.then_inc(g_high.sem, 1)

            def x_split(layer, when, kt):
                if layer == 0:
                    act.wait_ge(x_loaded.sem, at(x_loaded, layer, when, 16 * CT))
                else:
                    act.wait_ge(x_normed.sem, at(x_normed, layer, when, kt + 1))
                act.activation(x_hi[:, kt, :], x_in[:, kt, :], ACT.Copy).then_inc(x_high.sem, 1)

            def apply_norm(layer, when, ot):
                if ot == 0:
                    act.wait_ge(norm_ready.sem, at(norm_ready, layer, when, 1))
                act.activation(yb[:, ot, :], yb[:, ot, :], ACT.Identity, bias=norm_b[:, ot:ot + 1],
                               scale=norm_a[:, ot:ot + 1]).then_inc(y_scaled.sem, 1)

            def exps(layer, b, T):
                u, j = T // MT, T // 2
                act.wait_ge(s_made.sem, at(s_made, layer, b, T + 1))
                if T % MT == 0 and (layer or kind(b) != 0 or u >= 2):
                    act.wait_ge(o_made.sem, at(o_made, layer, b, u - 1))
                if T % 2 == 0 and not (kind(b) == 0 and layer == 0 and j < RING):
                    rest_wait(act, layer, b, j - RING)
                s = s_bank[T % 2]
                act.activation(p_f32[:, j % RING, T % 2, :], s[:, :], ACT.Exp, scale=EXP_SCALE)
                act.activation(p_hi[:, u % 2, T % MT, :], s[:, :], ACT.Exp, scale=EXP_SCALE).then_inc(p_made.sem, 1)

            def batch(layer, b):
                first = kind(b) == 0
                for p in range(PAIRS):
                    evict = evictions(first, p)
                    for t in range(SLOTS):
                        T = p * SLOTS + t
                        for item in evict[t]:
                            if item == ("proj", 0, 0):
                                act.wait_ge(y_stored.sem, at(y_stored, layer, b, 0))
                            high(layer, b, item, (p + 1) % PAIRS, (p + 1) % 2)
                        if p == NEXT_X_PAIR and t in NEXT_X_SLOTS:
                            if NEXT_X_SLOTS[t] == 0:
                                act.wait_ge(g_made.sem, at(g_made, layer, b, index(layer, b, ("v", p, 1)) + 1))
                            x_split(layer, b, NEXT_X_SLOTS[t])
                        if layer == 0 and p == 1 and not first and t in APPLY_SLOTS:
                            apply_norm(layer, b, APPLY_SLOTS[t])
                        exps(layer, b, T)

            act.wait_ge(const_ready, 1)
            act.wait_ge(params_ready, 1)
            for layer in range(2):
                if layer == 1:
                    act.wait_ge(g_made.sem, at(g_made, layer, "lead", 0))
                for kt in range(CT):
                    act.wait_ge(w_loaded[kt].sem, at(w_loaded[kt], layer, "lead", 32))
                    act.activation(w_hi[:, kt, :], w_in[:, kt % 2, :], ACT.Copy, scale=WEIGHT_SCALE).then_inc(w_high.sem, 1)
                for kt in range(CT):
                    x_split(layer, "lead", kt)
                for item in ORDER[layer]["lead"]:
                    high(layer, "lead", item, 0, 0)
                batch(layer, 0)
                with act.Fori(1, NB) as b:
                    batch(layer, b)
                act.wait_ge(y_stored.sem, at(y_stored, layer, "tail", 0))
                for item in HIGHS[layer]["tail"]:
                    high(layer, "tail", item, 0, 0)
                if layer == 0:
                    for ot in range(CT):
                        apply_norm(layer, "tail", ot)

        @block.vector
        def _(dve):
            def low(layer, when, item, p1, st):
                what, a, n = item
                dve.wait_ge(g_high.sem, at(g_high, layer, when, high_index(layer, when, item) + 1))
                g = bank_of(layer, when, item)
                cols = slice((n % 2) * COLS, (n % 2 + 1) * COLS)
                if what == "qk":
                    c = (n // 2) * CT + p1
                    upper, lower = ((qa, qb), (ka, ka))[n // 2]
                    for h in range(2):
                        rows = own(h) if n < 2 else own(1 - h)
                        last = dve.scalar_tensor_tensor(out=lower[rows, st, h, cols], in0=g[own(h), :],
                                                        scalar=biases[own(h), layer, c:c + 1],
                                                        in1=upper[own(h), st, h, cols], op0=ALU.add, op1=ALU.subtract)
                elif what == "v":
                    last = dve.tensor_tensor(v[:, st, 4 * n:4 * n + 4, :, VL:VL + HALF],
                                             g[:, :].rearrange("p (m h d) -> p m h d", m=4, h=2),
                                             v[:, st, 4 * n:4 * n + 4, :, 0:HALF], ALU.subtract)
                elif what == "turn":
                    last = dve.scalar_tensor_tensor(out=o_lo[:, a, cols], in0=g[:, :],
                                                    scalar=biases[:, layer, 2 * CT + a:2 * CT + a + 1],
                                                    in1=o_hi[:, a, cols], op0=ALU.add, op1=ALU.subtract)
                elif layer == 0:
                    last = dve.bn_stats(bn[:, a, n, :], yb[:, a, cols])
                else:
                    if a == 0 and n == 0:
                        dve.wait_ge(res_loaded.sem, at(res_loaded, layer, when, 0))
                    dve.tensor_tensor(yb[:, a, cols], yb[:, a, cols], x_res[:, a, cols], ALU.add)\
                        .then_inc(res_added.sem, 1)
                    last = dve.engine_nop()
                last.then_inc(g_free.sem, 1)

            def max_read_out(layer, when, n0, n):
                h, k = MAX_ORDER[n]
                dve.wait_ge(max_made.sem, at(max_made, layer, when, n0 + n + 1))
                m = m_bank[n % 2]
                if k is None:
                    dve.tensor_copy(shift_rows[:, h, :], m[0:MT, 0:HALF].bitcast(F16)).then_inc(max_read.sem, 1)
                else:
                    dve.tensor_reduce(maxes[:, h, k:k + 1], m[:, :], AX.X, ALU.max).then_inc(max_read.sem, 1)

            def make_shift(layer, when, n0, h):
                n = N_B - 1 if h else N_MAX - 1
                dve.wait_ge(max_read.sem, at(max_read, layer, when, n0 + n))
                dve.tensor_tensor(row_max[:, h, :], maxes[:, h, 0:MT], maxes[:, h, MT:2 * MT], ALU.max)\
                    .then_inc(max_joined.sem, 1)
                dve.wait_ge(max_joined.sem, at(max_joined, layer, when, shifts_until(n0, h)))
                dve.tensor_scalar(shift[:, h, :], row_max[:, h, :], -1.0 / SHIFT_UNIT, SHIFT_BONUS, ALU.mult, ALU.add)\
                    .then_inc(shift_ready.sem, 1)

            def divide(layer, when, u):
                h, nh = (u // 2) % 2, u % 2
                dve.wait_ge(o_made.sem, at(o_made, layer, when, u + 1))
                if u % 4 == 0 and u:
                    dve.wait_ge(g_made.sem, at(g_made, layer, when, index(layer, when, ("turn", u // 4 - 1, 1)) + 1))
                if u == 0 and kind(when) != 0:
                    dve.wait_ge(g_made.sem, at(g_made, layer, when, index(layer, when, ("turn", PAIRS - 1, 1)) + 1))
                o = o_bank[u % 2][:, 0:QT * (HALF + 1)].rearrange("p (q d) -> p q d", d=HALF + 1)
                dve.reciprocal(recip[:, u % 2, :], o[:, :, HALF]).then_inc(o_recip.sem, 1)
                dve.wait_ge(o_recip.sem, at(o_recip, layer, when, u + 1))
                dve.tensor_tensor(o_pair[:, nh * QT:(nh + 1) * QT, own(h)], o[:, :, 0:HALF],
                                  recip[:, u % 2, :].unsqueeze(2).to_broadcast([P, QT, HALF]), ALU.mult)\
                    .then_inc(o_read.sem, 1)

            def x_normalise(layer, when, kt, which):
                dve.wait_ge(x_loaded.sem, at(x_loaded, layer, when, 16 * CT))
                dve.tensor_scalar(x_in[:, kt, :], x_in[:, kt, :], next_a[:, which, kt:kt + 1].rearrange("p b o -> p (b o)"),
                                  next_b[:, which, kt:kt + 1].rearrange("p b o -> p (b o)"), ALU.mult, ALU.add)\
                    .then_inc(x_normed.sem, 1)

            def x_rest(layer, when, kt):
                dve.wait_ge(x_high.sem, at(x_high, layer, when, kt + 1))
                dve.tensor_tensor(x_lo[:, kt, :], x_in[:, kt, :], x_hi[:, kt, :], ALU.subtract).then_inc(x_low.sem, 1)

            class Norm:

                def __init__(self, layer, when):
                    self.layer, self.when, self.n = layer, when, 0

                def link(self, ins):
                    self.n += 1
                    ins.then_inc(links.sem, 1)
                    dve.wait_ge(links.sem, at(links, self.layer, self.when, self.n))

                def moments(self, which):
                    layer, when = self.layer, self.when
                    if which == 0:
                        dve.wait_ge(g_free.sem, at(g_free, layer, when, index(layer, when, ("proj", CT - 1, NH - 1)) + 1))
                    dve.memset(tmp[:, :], 0.0)
                    for ot in range(CT):
                        last = dve.bn_aggr(mv[:, ot, :], bn[:, ot, :, :].rearrange("p a s -> p (a s)"))
                    self.link(last)
                    dve.tensor_copy(gs[:, 0:CT], mv[:, :, 0])
                    self.link(dve.tensor_tensor(tmp[:, :], mv[:, :, 0], mv[:, :, 0], ALU.mult))
                    dve.tensor_tensor(gs[:, CT:2 * CT], tmp[:, :], mv[:, :, 1], ALU.add).then_inc(stats_ready.sem, 1)

                def variance(self, which):
                    layer, when = self.layer, self.when
                    item = ("norm", which, 0)
                    dve.wait_ge(g_made.sem, at(g_made, layer, when, index(layer, when, item) + 1))
                    dve.tensor_copy(gm[:, :], bank_of(layer, when, item)[:, 0:2 * CT]).then_inc(g_free.sem, 1)
                    dve.wait_ge(g_free.sem, at(g_free, layer, when, index(layer, when, item) + 1))
                    self.link(dve.tensor_tensor(tmp[:, :], gm[:, 0:CT], gm[:, 0:CT], ALU.mult))
                    self.link(dve.scalar_tensor_tensor(out=tmp[:, :], in0=gm[:, CT:2 * CT], scalar=1.0, in1=tmp[:, :],
                                                       op0=ALU.mult, op1=ALU.subtract))
                    dve.tensor_scalar(var[:, :], tmp[:, :], EPS, None, ALU.add).then_inc(var_ready.sem, 1)

                def factors(self, which, place):
                    a_out, b_out = (norm_a[:, :], norm_b[:, :]) if which == 0 else \
                        (next_a[:, place, :].rearrange("p b o -> p (b o)"), next_b[:, place, :].rearrange("p b o -> p (b o)"))
                    dve.wait_ge(rstd_ready.sem, at(rstd_ready, self.layer, self.when, which + 1))
                    self.link(dve.tensor_tensor(a_out, rstd[:, :], affine[:, 2 * which, :], ALU.mult))
                    self.link(dve.tensor_tensor(tmp[:, :], gm[:, 0:CT], a_out, ALU.mult))
                    dve.tensor_tensor(b_out, affine[:, 2 * which + 1, :], tmp[:, :], ALU.subtract).then_inc(norm_ready.sem, 1)

                def add(self, ot):
                    layer, when = self.layer, self.when
                    if ot == 0:
                        dve.wait_ge(res_loaded.sem, at(res_loaded, layer, when, 0))
                    dve.wait_ge(y_scaled.sem, at(y_scaled, layer, when, ot + 1))
                    dve.tensor_tensor(yb[:, ot, :], yb[:, ot, :], x_res[:, ot, :], ALU.add).then_inc(res_added.sem, 1)
                    dve.wait_ge(res_added.sem, at(res_added, layer, when, ot + 1))
                    for nh in range(NH):
                        last = dve.bn_stats(bn[:, ot, nh, :], yb[:, ot, nh * COLS:(nh + 1) * COLS])
                    if ot == CT - 1:
                        self.link(last)

            def batch(layer, b, before, following):
                first = kind(b) == 0
                norm = Norm(layer, b)
                for p in range(PAIRS):
                    evict = evictions(first, p)
                    for t in range(SLOTS):
                        T = p * SLOTS + t
                        if t == SHIFT_A_CHAIN:
                            make_shift(layer, b, p * N_MAX, 0)
                        if t == SHIFT_B_CHAIN:
                            make_shift(layer, b, p * N_MAX, 1)
                        for n in MAX_SLOTS[t]:
                            max_read_out(layer, b, p * N_MAX, n)
                        j = T // 2 - 1
                        if T % 2 == 0 and (j >= 0 or not first) and j % (MT // 2) in SHARE_V:
                            rest_of_exp(dve, layer, b, j, rest_v)
                        if T % MT == 0 and (T >= 2 * MT or not first):
                            divide(layer, b, T // MT - 2)
                        for item in evict[t]:
                            low(layer, b, item, (p + 1) % PAIRS, (p + 1) % 2)
                        if layer == 1 and p == NEXT_X_PAIR and t in NORMALISE_SLOTS:
                            x_normalise(layer, b, NORMALISE_SLOTS[t], following)
                        if T - 1 - NEXT_X_PAIR * SLOTS in NEXT_X_SLOTS:
                            x_rest(layer, b, NEXT_X_SLOTS[T - 1 - NEXT_X_PAIR * SLOTS])
                        if layer == 0 and not first and p in (1, 2):
                            if t == STATS_SLOT:
                                norm.moments(p - 1)
                            if t == VAR_SLOT:
                                norm.variance(p - 1)
                            if t == FACTOR_SLOT:
                                norm.factors(p - 1, before)
                            if p == 1 and t - 1 in APPLY_SLOTS:
                                norm.add(APPLY_SLOTS[t - 1])
                assert norm.n == (0 if first else links.per[layer]), norm.n

            dve.wait_ge(const_ready, 1)
            dve.wait_ge(params_in, 96)
            dve.tensor_scalar(biases[:, 1, 0:3 * CT], biases[:, 1, 0:3 * CT], WEIGHT_SCALE, None, ALU.mult)\
                .then_inc(params_ready, 1)
            dve.wait_ge(params_ready, 1)
            dve.engine_nop().then_inc(y_stored.sem, 1)

            for layer in range(2):
                for kt in range(CT):
                    dve.wait_ge(w_high.sem, at(w_high, layer, "lead", kt + 1))
                    dve.scalar_tensor_tensor(out=w_lo[:, kt, :], in0=w_in[:, kt % 2, :], scalar=WEIGHT_SCALE,
                                             in1=w_hi[:, kt, :], op0=ALU.mult, op1=ALU.subtract).then_inc(w_low.sem, 1)
                if layer == 1:
                    for kt in range(CT):
                        x_normalise(layer, "lead", kt, slice(0, 1))
                for kt in range(CT):
                    x_rest(layer, "lead", kt)
                for item in ORDER[layer]["lead"]:
                    low(layer, "lead", item, 0, 0)
                for n in range(N_B, N_MAX):
                    if n == N_MAX - 1:
                        make_shift(layer, "lead", -N_B, 0)
                    max_read_out(layer, "lead", -N_B, n)
                batch(layer, 0, None, slice(1, 2))
                with dve.Fori(1, NB) as b:
                    batch(layer, b, bass.ds(b - 1, 1), bass.ds((b + 1) % NB, 1))
                if (MT // 2 - 1) in SHARE_V:
                    rest_of_exp(dve, layer, "tail", -1, rest_v)
                divide(layer, "tail", -2)
                divide(layer, "tail", -1)
                for item in HIGHS[layer]["tail"]:
                    low(layer, "tail", item, 0, 0)
                if layer == 0:
                    norm = Norm(layer, "tail")
                    norm.moments(0)
                    norm.variance(0)
                    norm.factors(0, None)
                    for ot in range(CT):
                        norm.add(ot)
                    norm.moments(1)
                    norm.variance(1)
                    norm.factors(1, slice(NB - 1, NB))


_INS = ["x", "L0_conv_w_qkv", "L0_conv_w_proj", "L0_conv_gamma", "L0_conv_beta", "L1_conv_norm_w", "L1_conv_norm_b",
        "L1_conv_qkv_w", "L1_conv_qkv_b", "L1_conv_proj_w", "L1_conv_proj_b"]
_TURNED = {"L0_conv_w_qkv", "L0_conv_w_proj", "L1_conv_qkv_w", "L1_conv_proj_w"}


def kernel(**inputs):
    import numpy as _np
    import concourse.bacc as _bacc
    from concourse import mybir as _mybir
    from concourse.bass_utils import run_bass_kernel_spmd as _run

    nc = _bacc.Bacc("TRN2", target_bir_lowering=False, num_devices=1)
    arrays, args = {}, []
    for name in _INS:
        a = _np.asarray(inputs[name])
        if name == "x":
            b, c, h, w = a.shape
            a = a.reshape(b, c, h * w)
        if name in _TURNED:
            a = a.T
        if a.ndim == 1:
            a = a.reshape(-1, 128).T
        a = _np.ascontiguousarray(a)
        arrays[f"in_{name}_dram"] = a
        args.append(nc.dram_tensor(f"in_{name}_dram", a.shape, _mybir.dt.from_np(a.dtype), kind="ExternalInput").ap())
    args.append(nc.dram_tensor("out_0_dram", (b, c, h * w), _mybir.dt.float32, kind="ExternalOutput").ap())
    two_attention_blocks(nc, *args)
    r = _run(nc, [arrays], core_ids=[0])
    return _np.asarray(r.results[0]["out_0_dram"]).reshape(b, c, h, w)
```

```python
import math
from contextlib import ExitStack

import concourse.bass as bass
from concourse import mybir

F32 = mybir.dt.float32
F16 = mybir.dt.float16
ALU = mybir.AluOpType
ACT = mybir.ActivationFunctionType
AX = mybir.AxisListType

P = 128
HALF = 64
COLS = 512
EPS = 1e-5
WEIGHT_SCALE = 16.0
SHIFT_UNIT = 1024.0
HEADROOM = 256.0


class Stage:

    def __init__(self, name, layer, finish, ahead, here=None, before=None, following=None, first=0):
        self.name, self.layer, self.finish, self.ahead = name, layer, finish, ahead
        self.here, self.before, self.following = here, before, following
        self.first = first

    def layer_of(self, p):
        return self.ahead if p == 3 else self.layer


class Tally:

    def __init__(self, sem, counts, rounds):
        self.sem, self.counts, self.start, self.end = sem, counts, {}, 0
        for name, count in counts.items():
            self.start[name] = self.end
            self.end += rounds[name] * count


def at(tally, stage, n):
    count = tally.counts[stage.name]
    value = tally.start[stage.name] + n
    if stage.first and count:
        return value - stage.first * count + stage.here * count
    return value


def one(i):
    return slice(i, i + 1) if isinstance(i, int) else bass.ds(i, 1)


SLOTS = 32
QK_SLOTS = range(1, 13)
TURN_SLOTS = {13: 0, 15: 1}
NORM_SLOT = 14
QUEUE_FIRST = (16, 16, 16, 16)
V_LAST = (30, 29, 22, 29)
PROJ_LAST = 30
MAX_B_SLOTS, SHIFT_B_CHAIN = 12, 12
MAX_A_FIRST, SHIFT_A_CHAIN = 13, 27
PV_OFFSETS = {2: 0, 4: 1, 5: 2, 7: 3}
NEXT_X_PAIR, NEXT_X_SLOTS = 2, {23: 0, 27: 1, 30: 2, 33: 3}
NORMALISE_SLOTS = {8: 0, 10: 1, 12: 2, 14: 3}
STATS_SLOTS, VAR_SLOT, FACTOR_SLOT = (2, 4), 15, 18
APPLY_SLOTS = {19: 0, 23: 1, 27: 2, 31: 3}
WEIGHT_SLOTS = {23: 0, 24: 1, 26: 2, 28: 3}
PROJ_WEIGHT_SLOTS = {20: 0, 22: 1, 24: 2, 26: 3}


def max_order():
    tiles = [[(h, k) for k in range(16)] for h in range(2)]
    return tiles[1] + [(1, None)] + tiles[0] + [(0, None)]


def max_slots():
    found = {t: [] for t in range(SLOTS)}
    for n in range(16):
        found[n * MAX_B_SLOTS // 16].append(n)
    found[SHIFT_B_CHAIN + 1].append(16)
    for n in range(16):
        found[MAX_A_FIRST + n * (SHIFT_A_CHAIN - MAX_A_FIRST) // 16].append(17 + n)
    found[SHIFT_A_CHAIN + 1].append(33)
    return found


def spread(costs, first, last):
    total, done, n, out = sum(costs), 0.0, 0, {}
    for t in range(first, last + 1):
        k = n
        while n < len(costs) and done < total * (t + 1 - first) / (last + 1 - first) - 1e-9:
            done += costs[n]
            n += 1
        out[t] = (k, n)
    assert n == len(costs)
    return out


def two_attention_blocks(
    nc: bass.Bass,
    x, w_qkv0, w_proj0, gamma0, beta0, norm_w1, norm_b1, w_qkv1, qkv_b1, w_proj1, proj_b1,
    out,
):
    NB, C, N = x.shape
    CT = C // P
    PAIRS = C // P
    MT = N // P
    NH = N // COLS
    QT = COLS // P
    WCOLS = 4 * C
    BSLOTS = PAIRS * SLOTS
    UNITS = 2 * NH * PAIRS
    RING = 4
    GROUP = 64
    EXP_SCALE = float(HALF) ** -0.5 / WEIGHT_SCALE ** 2
    VW = 136
    VL = 72
    SHIFT_BONUS = math.log(HEADROOM) / EXP_SCALE / SHIFT_UNIT
    assert (CT, PAIRS, MT, NH, 2 * NH * MT) == (4, 4, 8, 2, SLOTS)

    MAX_ORDER, MAX_SLOTS = max_order(), max_slots()
    N_MAX = len(MAX_ORDER)
    N_B = N_MAX // 2

    LEAD = Stage("lead", None, None, 0, following=0)
    FIRST0 = Stage("first0", 0, None, 0, here=0, following=1)
    LAST0 = Stage("last0", 0, 0, 1, here=NB - 1, before=NB - 2, following=0)
    FIRST1 = Stage("first1", 1, 0, 1, here=0, before=NB - 1, following=1)
    LAST1 = Stage("last1", 1, 1, None, here=NB - 1, before=NB - 2)
    TAIL = Stage("tail", None, 1, None, before=NB - 1)

    def middle(layer, b):
        return Stage(f"middle{layer}", layer, layer, layer, here=b, before=b - 1, following=b + 1, first=1)

    STAGES = [LEAD, FIRST0, middle(0, 1), LAST0, FIRST1, middle(1, 1), LAST1, TAIL]
    ROUNDS = {s.name: NB - 2 if s.first else 1 for s in STAGES}
    QKV_STAGES = ("lead", "last0")
    PROJ_STAGES = ("first0", "first1")
    assert NB >= 3

    def step_items(s, p):
        looks = s.layer_of(p) is not None
        items = [("qk", p, k) for k in range(4)] if looks else []
        if p or s.finish is not None:
            items += [("turn", (p - 1) % PAIRS, 0)]
        if s.finish == 0 and p in (1, 2):
            items += [("norm", p - 1, 0)]
        if p or s.finish is not None:
            items += [("turn", (p - 1) % PAIRS, 1)]
        if looks:
            items += [("v", p, 0), ("v", p, 1)]
        if p == 0 and s.finish is not None:
            items += [("proj", ot, nh) for ot in range(CT) for nh in range(NH)]
        return items

    def items_of(s):
        if s.name == "lead":
            return [("qk", -1, k) for k in range(4)] + [("v", -1, 0), ("v", -1, 1)]
        if s.name == "tail":
            return [("turn", PAIRS - 1, 0), ("turn", PAIRS - 1, 1)] + \
                [("proj", ot, nh) for ot in range(CT) for nh in range(NH)]
        return [it for p in range(PAIRS) for it in step_items(s, p)]

    ORDER = {s.name: items_of(s) for s in STAGES}
    INDEX = {k: {it: n for n, it in enumerate(ORDER[k])} for k in ORDER}
    HIGHS = {k: {it: n for n, it in enumerate(i for i in ORDER[k] if i[0] != "norm")} for k in ORDER}
    assert all(len(ORDER[k]) % 2 == 0 for k in ORDER)

    def index(s, item):
        return INDEX[s.name][item]

    def high_index(s, item):
        return HIGHS[s.name][item]

    def queue_slots(s, p):
        items = [("v", p, 0), ("v", p, 1)] if s.layer_of(p) is not None else []
        last = V_LAST[p]
        if p == 0 and s.finish is not None:
            items += [("proj", ot, nh) for ot in range(CT) for nh in range(NH)]
            last = PROJ_LAST
        flat = [(it, k) for it in items for k in range(4 * 3 * CT if it[0] == "v" else 3 * CT)]
        found = {}
        for t, (k0, k1) in spread([1.0 if it[0] == "v" else 4.0 for it, _ in flat], QUEUE_FIRST[p], last).items():
            parts = {}
            for it, k in flat[k0:k1]:
                parts.setdefault(it, []).append(k)
            found[t] = [(it, ks[0], ks[-1] + 1) for it, ks in parts.items()]
        return found

    def evictions(s, p):
        found = {t: [] for t in range(SLOTS)}
        if s.layer_of(p) is not None:
            for k in range(4):
                found[QK_SLOTS[3 * k + 2] + 1].append(("qk", p, k))
        if p or s.finish is not None:
            for t, half in TURN_SLOTS.items():
                found[t + 1].append(("turn", (p - 1) % PAIRS, half))
        for t, parts in queue_slots(s, p).items():
            for it, _, k1 in parts:
                if k1 == (4 * 3 * CT if it[0] == "v" else 3 * CT):
                    found[t + 1].append(it)
        return found

    def max_uses(s, p, t):
        return [n for n in MAX_SLOTS[t] if n < N_B or s.layer_of(p) is not None]

    with ExitStack() as ctx:
        def sb(name, shape, dt):
            return ctx.enter_context(nc.sbuf_tensor(name, shape, dt))

        def bank(name):
            return ctx.enter_context(nc.psum_tensor(name, [P, COLS], F32))

        def tally(name, count):
            return Tally(ctx.enter_context(nc.semaphore(name)), {s.name: count(s) for s in STAGES}, ROUNDS)

        y_dram = nc.dram_tensor("y_scratch", (NB, C, N), F32, kind="Internal").ap()

        w_hi = sb("w_hi", [P, CT, WCOLS], F16)
        w_lo = sb("w_lo", [P, CT, WCOLS], F16)
        x_in = sb("x_in", [P, CT, N], F32)
        x_res = sb("x_res", [P, CT, N], F32)
        x_hi = sb("x_hi", [P, CT, N], F16)
        x_lo = sb("x_lo", [P, CT, N], F16)
        qa = sb("qa", [P, 2, 2, N], F16)
        qb = sb("qb", [P, 2, 2, N], F16)
        ka = sb("ka", [P, 2, 2, N], F16)
        kb = sb("kb", [P, 2, 2, N], F16)
        v = sb("v", [P, 2, MT, 2, VW], F16)
        p_f32 = sb("p_f32", [P, RING, 2, COLS], F32)
        p_hi = sb("p_hi", [P, 2, MT, COLS], F16)
        p_lo = sb("p_lo", [P, 2, MT, COLS], F16)
        o_pair = sb("o_pair", [P, MT, P], F32)
        o_hi = sb("o_hi", [P, CT, N], F16)
        o_lo = sb("o_lo", [P, CT, N], F16)
        yb = sb("yb", [P, CT, N], F32)
        w_in = [t[:, :, :].rearrange("p (a b) n -> p a (b n)", a=2)[:, a, 0:3 * C] for t in (yb, x_res) for a in range(2)]
        ident = sb("ident", [P, P], F32)
        ident16 = sb("ident16", [P, P], F16)
        group_mean = sb("group_mean", [P, P], F32)
        biases = sb("biases", [P, 2, 4 * CT], F32)
        affine = sb("affine", [P, 4, CT], F32)
        maxes = sb("maxes", [P, 2, 2 * MT], F32)
        row_max = sb("row_max", [P, 2, MT], F32)
        shift = sb("shift", [P, 2, MT], F16)
        shift_rows = sb("shift_rows", [MT, 2, P], F16)
        recip = sb("recip", [P, 2, QT], F32)
        bn = sb("bn", [P, CT, NH, 6], F32)
        mv = sb("mv", [P, CT, 2], F32)
        gs = sb("gs", [P, 2 * CT], F32)
        gm = sb("gm", [P, 2 * CT], F32)
        var = sb("var", [P, CT], F32)
        rstd = sb("rstd", [P, CT], F32)
        tmp = sb("tmp", [P, CT], F32)
        minus_half = sb("minus_half", [P, CT], F32)
        norm_a = sb("norm_a", [P, CT], F32)
        norm_b = sb("norm_b", [P, CT], F32)
        next_a = sb("next_a", [P, NB, CT], F32)
        next_b = sb("next_b", [P, NB, CT], F32)

        s_bank = [bank("s_bank0"), bank("s_bank1")]
        m_bank = [bank("m_bank0"), bank("m_bank1")]
        o_bank = [bank("o_bank0"), bank("o_bank1")]
        g_bank = [bank("g_bank0"), bank("g_bank1")]

        const_ready = ctx.enter_context(nc.semaphore("const_ready"))
        const_step = ctx.enter_context(nc.semaphore("const_step"))
        params_in = ctx.enter_context(nc.semaphore("params_in"))
        params_ready = ctx.enter_context(nc.semaphore("params_ready"))

        def attends(s, n):
            return n if s.layer is not None else 0

        def begins(s, n):
            return n if s.ahead is not None else 0

        def finishes(s, n, layers=(0, 1)):
            return n if s.finish in layers else 0

        def looks(s, n):
            if s.name == "lead":
                return n
            return attends(s, (PAIRS if s.ahead is not None else PAIRS - 1) * n)

        brings = QKV_STAGES + PROJ_STAGES
        w_loaded = [tally(f"w_loaded{k}", lambda s: 16 if s.name in brings else 0) for k in range(CT)]
        others_loaded = [tally(f"others_loaded{k}", lambda s: 16 if s.name == "lead" else 0) for k in range(CT)]
        chunks = {s.name: 2 * CT if s.name == "lead" else CT if s.name in brings else 0 for s in STAGES}
        w_high = tally("w_high", lambda s: chunks[s.name])
        w_low = tally("w_low", lambda s: chunks[s.name])
        x_loaded = [tally(f"x_loaded{k}", lambda s: begins(s, 16)) for k in range(CT)]
        x_normed = tally("x_normed", lambda s: CT if s.ahead == 1 else 0)
        x_high = tally("x_high", lambda s: begins(s, CT))
        x_low = tally("x_low", lambda s: begins(s, CT))
        g_made = tally("g_made", lambda s: len(ORDER[s.name]))
        g_free = tally("g_free", lambda s: len(ORDER[s.name]))
        g_high = tally("g_high", lambda s: len(HIGHS[s.name]))
        q_copied = tally("q_copied", lambda s: looks(s, 32))
        k_copied = tally("k_copied", lambda s: looks(s, 32))
        max_made = tally("max_made", lambda s: looks(s, N_B) + attends(s, PAIRS * N_B))
        max_read = tally("max_read", lambda s: looks(s, N_B) + attends(s, PAIRS * N_B))
        max_joined = tally("max_joined", lambda s: looks(s, 1) + attends(s, PAIRS))
        shift_ready = tally("shift_ready", lambda s: looks(s, 1) + attends(s, PAIRS))
        shift_placed = [tally("shift_placed0", lambda s: looks(s, 16)),
                        tally("shift_placed1", lambda s: attends(s, 16 * PAIRS))]
        s_made = tally("s_made", lambda s: attends(s, BSLOTS))
        p_made = tally("p_made", lambda s: attends(s, BSLOTS))
        p_rest = tally("p_rest", lambda s: attends(s, BSLOTS // 2))
        o_made = tally("o_made", lambda s: attends(s, UNITS))
        o_recip = tally("o_recip", lambda s: attends(s, UNITS))
        o_read = tally("o_read", lambda s: attends(s, UNITS))
        res_loaded = tally("res_loaded", lambda s: attends(s, 16 * CT))
        ADDS = [CT, CT * NH]
        res_added = tally("res_added", lambda s: 0 if s.finish is None else ADDS[s.finish])
        y_scaled = tally("y_scaled", lambda s: finishes(s, CT, (0,)))
        y_stored = tally("y_stored", lambda s: 1 if s.name == "lead" else finishes(s, 16 * CT))
        stats_ready = tally("stats_ready", lambda s: finishes(s, 2, (0,)))
        var_ready = tally("var_ready", lambda s: finishes(s, 2, (0,)))
        rstd_ready = tally("rstd_ready", lambda s: finishes(s, 2, (0,)))
        norm_ready = tally("norm_ready", lambda s: finishes(s, 2, (0,)))
        links = tally("links", lambda s: finishes(s, 13, (0,)))

        block = ctx.enter_context(nc.Block())

        def of_pairs(t, p0, p1):
            return t[:, 0:3 * C].rearrange("p (a c) -> p a c", a=3)[:, :, p0 * P:p1 * P]

        def own(h):
            return slice(h * HALF, (h + 1) * HALF)

        def other_row(h):
            return HALF if h == 0 else 0

        def bank_of(s, item):
            return g_bank[index(s, item) % 2]

        def layer_of(s, item):
            if item[0] in ("qk", "v"):
                return s.layer_of(item[1]) if item[1] >= 0 else s.ahead
            if item[0] == "turn" and item[1] < PAIRS - 1:
                return s.layer
            return s.finish

        def shifts_until(n0, h):
            return 1 if n0 < 0 else 2 * (n0 // N_MAX) + 2 - h

        @block.sync
        def _(sp):
            def copy_q(s, p, st):
                sp.wait_ge(g_high.sem, at(g_high, s, high_index(s, ("qk", p, 1)) + 1))
                for h in range(2):
                    sp.dma_start(qa[own(1 - h), st, h, :], qa[own(h), st, h, :]).then_inc(q_copied.sem, 16)

            def copy_k(s, p, st):
                sp.wait_ge(g_high.sem, at(g_high, s, high_index(s, ("qk", p, 3)) + 1))
                for h in range(2):
                    sp.dma_start(kb[own(h), st, h, :], ka[own(h), st, h, :]).then_inc(k_copied.sem, 16)

            def place_shift(s, n, st, h):
                sp.wait_ge(max_read.sem, at(max_read, s, n))
                r = other_row(h)
                sp.dma_start(qb[r:r + 1, st, h, :].rearrange("o (a n) -> o a n", a=MT), shift_rows[:, h, :])\
                    .then_inc(shift_placed[h].sem, 16)

            def rows_of(tensor, i, t):
                return tensor[one(i), t * P:(t + 1) * P, :].rearrange("b p n -> p (b n)")

            def load_x(s, kt):
                sp.dma_start(x_in[:, kt, :], rows_of(SOURCE[s.ahead], s.following, kt)).then_inc(x_loaded[kt].sem, 16)

            def store_y(s):
                for ot in range(CT):
                    sp.wait_ge(res_added.sem, at(res_added, s, (ot + 1) * ADDS[s.finish] // CT))
                    sp.dma_start(rows_of((y_dram, out)[s.finish], s.before, ot), yb[:, ot, :]).then_inc(y_stored.sem, 16)

            def load_qkv_weights(layer, kt):
                sp.dma_start(w_in[kt], (w_qkv0, w_qkv1)[layer][kt * P:(kt + 1) * P, :]).then_inc(w_loaded[kt].sem, 16)

            def batch(s):
                if s.ahead is not None:
                    sp.wait_ge(x_low.sem, at(x_low, s, 0))
                    if s.ahead == 1:
                        sp.wait_ge(y_stored.sem, at(y_stored, s, 0))
                    for kt in range(CT):
                        load_x(s, kt)
                for p in range(PAIRS):
                    st, next_pair = (p + 1) % 2, s.layer_of(p) is not None
                    if next_pair:
                        copy_q(s, p, st)
                    place_shift(s, p * N_MAX + N_B, p % 2, 1)
                    if next_pair:
                        copy_k(s, p, st)
                    if s.finish is not None and p == (2, 1)[s.finish]:
                        store_y(s)
                    if s.name in QKV_STAGES and p == 2:
                        sp.wait_ge(y_stored.sem, at(y_stored, s, 16 * CT))
                        sp.wait_ge(stats_ready.sem, at(stats_ready, s, 2))
                        for kt in range(CT):
                            load_qkv_weights(s.ahead, kt)
                    if p == PAIRS - 1:
                        if s.finish is not None:
                            sp.wait_ge(res_added.sem, at(res_added, s, ADDS[s.finish]))
                        if s.name in QKV_STAGES:
                            sp.wait_ge(w_low.sem, at(w_low, s, CT))
                        for ot in range(CT):
                            sp.dma_start(x_res[:, ot, :], rows_of(SOURCE[s.layer], s.here, ot)).then_inc(res_loaded.sem, 16)
                        if s.name in PROJ_STAGES:
                            if s.finish is not None:
                                sp.wait_ge(y_stored.sem, at(y_stored, s, 16 * CT))
                                sp.wait_ge(stats_ready.sem, at(stats_ready, s, 2))
                            for kt in range(CT):
                                sp.dma_start(yb[:, kt, 0:C], (w_proj0, w_proj1)[s.layer][kt * P:(kt + 1) * P, :])\
                                    .then_inc(w_loaded[kt].sem, 16)
                    if next_pair:
                        place_shift(s, (p + 1) * N_MAX, st, 0)

            SOURCE = (x, y_dram)
            for kt in range(CT):
                sp.dma_start(of_pairs(w_in[kt], 0, 1), of_pairs(w_qkv0[kt * P:(kt + 1) * P, :], 0, 1))\
                    .then_inc(w_loaded[kt].sem, 16)
                load_x(LEAD, kt)
            sp.dma_start(biases[:, 1, 0:3 * CT], qkv_b1).then_inc(params_in, 16)
            sp.dma_start(biases[:, 1, 3 * CT:4 * CT], proj_b1).then_inc(params_in, 16)
            for n, a in enumerate((gamma0, beta0, norm_w1, norm_b1)):
                sp.dma_start(affine[:, n, :], a).then_inc(params_in, 16)
            for kt in range(CT):
                sp.dma_start(of_pairs(w_in[kt], 1, PAIRS), of_pairs(w_qkv0[kt * P:(kt + 1) * P, :], 1, PAIRS))\
                    .then_inc(others_loaded[kt].sem, 16)
            copy_q(LEAD, -1, 0)
            copy_k(LEAD, -1, 0)
            place_shift(LEAD, N_MAX - N_B, 0, 0)
            batch(FIRST0)
            with sp.Fori(1, NB - 1) as b:
                batch(middle(0, b))
            batch(LAST0)
            batch(FIRST1)
            with sp.Fori(1, NB - 1) as b:
                batch(middle(1, b))
            batch(LAST1)
            store_y(TAIL)
            sp.wait_ge(y_stored.sem, y_stored.end)

        @block.gpsimd
        def _(pool):
            steps = [0]

            def step(ins):
                steps[0] += 1
                ins.then_inc(const_step, 1)
                pool.wait_ge(const_step, steps[0])

            for m in (ident, ident16):
                step(pool.memset(m[:, :], 0.0))
                step(pool.affine_select(out=m[:, :], in_=m[:, :], compare_op=ALU.not_equal, fill=1.0, base=0,
                                        pattern=[[-1, P]], channel_multiplier=1))
            step(pool.memset(group_mean[:, :], 0.0))
            for g in range(P // GROUP):
                step(pool.memset(group_mean[g * GROUP:(g + 1) * GROUP, g * GROUP:(g + 1) * GROUP], 1.0 / GROUP))
            for h in range(2):
                r = other_row(h)
                step(pool.memset(kb[own(1 - h), :, h, :], 0.0))
                step(pool.memset(kb[r:r + 1, :, h, :], SHIFT_UNIT))
                step(pool.memset(qb[own(1 - h), :, h, :], 0.0))
            for st in range(2):
                step(pool.memset(v[:, st, :, :, HALF:HALF + 1], 1.0))
            step(pool.memset(biases[:, 0, :], 0.0))
            pool.memset(minus_half[:, :], -0.5).then_inc(const_ready, 1)
            pool.wait_ge(const_ready, 1)

            def power(s, which):
                pool.wait_ge(var_ready.sem, at(var_ready, s, which + 1))
                pool.tensor_tensor(rstd[:, :], var[:, :], minus_half[:, :], ALU.pow).then_inc(rstd_ready.sem, 1)

            def batch(s):
                for j in range(BSLOTS // 2):
                    if s.finish == 0 and j in (1 * SLOTS // 2 + 8, 2 * SLOTS // 2 + 8):
                        power(s, j // (SLOTS // 2) - 1)
                    u, mt = (2 * j) // MT, (2 * j) % MT
                    pool.wait_ge(p_made.sem, at(p_made, s, 2 * j + 2))
                    pool.tensor_tensor(p_lo[:, u % 2, mt:mt + 2, :], p_f32[:, j % RING, :, :], p_hi[:, u % 2, mt:mt + 2, :],
                                       ALU.subtract).then_inc(p_rest.sem, 1)

            batch(FIRST0)
            with pool.Fori(1, NB - 1) as b:
                batch(middle(0, b))
            batch(LAST0)
            batch(FIRST1)
            with pool.Fori(1, NB - 1) as b:
                batch(middle(1, b))
            batch(LAST1)

        @block.tensor
        def _(pe):
            def claim(s, item):
                n = index(s, item)
                if s.name != "lead" or n >= 2:
                    pe.wait_ge(g_free.sem, at(g_free, s, n - 1))

            def qk_terms(p, which):
                w0 = (which // 2) * C + p * P
                cols = slice((which % 2) * COLS, (which % 2 + 1) * COLS)
                terms = []
                for kt in range(CT):
                    wh, wl = w_hi[:, kt, w0:w0 + P], w_lo[:, kt, w0:w0 + P]
                    terms += [(wh, x_hi[:, kt, cols]), (wh, x_lo[:, kt, cols]), (wl, x_hi[:, kt, cols])]
                return terms

            def v_terms(p, mt):
                w0 = 2 * C + p * P
                rows = slice(mt * P, (mt + 1) * P)
                terms = []
                for kt in range(CT):
                    wh, wl = w_hi[:, kt, w0:w0 + P], w_lo[:, kt, w0:w0 + P]
                    terms += [(x_hi[:, kt, rows], wh), (x_hi[:, kt, rows], wl), (x_lo[:, kt, rows], wh)]
                return terms

            def proj_terms(ot, nh):
                w0 = 3 * C + ot * P
                cols = slice(nh * COLS, (nh + 1) * COLS)
                terms = []
                for ct in range(CT):
                    wh, wl = w_hi[:, ct, w0:w0 + P], w_lo[:, ct, w0:w0 + P]
                    terms += [(wh, o_hi[:, ct, cols]), (wh, o_lo[:, ct, cols]), (wl, o_hi[:, ct, cols])]
                return terms

            def products(s, item, k0=0, k1=None, p1=0):
                what, a, n = item
                g = bank_of(s, item)
                if what == "v":
                    terms = [t for j in range(4) for t in v_terms(p1, 4 * n + j)]
                    areas = [g[:, j * P:(j + 1) * P] for j in range(4)]
                else:
                    terms = qk_terms(p1, n) if what == "qk" else proj_terms(a, n)
                    areas = [g[:, :]]
                run = len(terms) // len(areas)
                k1 = len(terms) if k1 is None else k1
                if k0 == 0:
                    claim(s, item)
                for k in range(k0, k1):
                    last = pe.matmul(areas[k // run], *terms[k], start=(k % run == 0), stop=(k % run == run - 1))
                if k1 == len(terms):
                    last.then_inc(g_made.sem, 1)

            def max_use(s, n0, n, st):
                h, k = MAX_ORDER[n]
                if s.name != "lead" or n >= N_B + 2:
                    pe.wait_ge(max_read.sem, at(max_read, s, n0 + n - 1))
                m = m_bank[n % 2]
                if k is None:
                    pe.wait_ge(shift_ready.sem, at(shift_ready, s, shifts_until(n0, h)))
                    pe.transpose(m[0:MT, 0:HALF].bitcast(F16), shift[:, h, :], ident16[:, :]).then_inc(max_made.sem, 1)
                else:
                    nt, mh = k % MT, k // MT
                    pe.matmul(m[:, :], qa[:, st, h, nt * P:(nt + 1) * P], ka[:, st, h, mh * COLS:(mh + 1) * COLS],
                              start=True, stop=True).then_inc(max_made.sem, 1)

            def turn_output(s, p, half):
                item = ("turn", p, half)
                claim(s, item)
                pe.wait_ge(o_read.sem, at(o_read, s, 0 if p == PAIRS - 1 else 4 * (p + 1)))
                g = bank_of(s, item)
                for j in range(QT):
                    last = pe.transpose(g[:, j * P:(j + 1) * P], o_pair[:, half * QT + j, :], ident[:, :])
                last.then_inc(g_made.sem, 1)

            def average(s, which):
                claim(s, ("norm", which, 0))
                pe.wait_ge(stats_ready.sem, at(stats_ready, s, which + 1))
                pe.matmul(bank_of(s, ("norm", which, 0))[:, 0:2 * CT], group_mean[:, :], gs[:, :],
                          start=True, stop=True).then_inc(g_made.sem, 1)

            def scores(s, T):
                p, h, nh, mt = T // SLOTS, (T % SLOTS) // (NH * MT), (T // MT) % NH, T % MT
                st = p % 2
                bank = s_bank[T % 2]
                if s.name != "first0" or T >= 2:
                    pe.wait_ge(p_made.sem, at(p_made, s, T - 1))
                if T % (NH * MT) == 0:
                    pe.wait_ge(shift_placed[h].sem, at(shift_placed[h], s, 16 * (p + h)))
                if T % SLOTS == 0:
                    pe.wait_ge(k_copied.sem, at(k_copied, s, 32 * p))
                keys, queries = slice(mt * P, (mt + 1) * P), slice(nh * COLS, (nh + 1) * COLS)
                pe.matmul(bank[:, :], ka[:, st, h, keys], qa[:, st, h, queries], start=True, stop=False)
                pe.matmul(bank[:, :], kb[:, st, h, keys], qb[:, st, h, queries], start=False, stop=True)\
                    .then_inc(s_made.sem, 1)

            def weighted_sum(s, u, k):
                h, st, buf = (u // 2) % 2, (u // 4) % 2, u % 2
                o = o_bank[buf]
                if k == 0:
                    pe.wait_ge(p_rest.sem, at(p_rest, s, (MT // 2) * (u + 1)))
                    if s.name != "first0" or u >= 2:
                        pe.wait_ge(o_read.sem, at(o_read, s, u - 1))
                    if u % 4 == 0:
                        pe.wait_ge(g_free.sem, at(g_free, s, index(s, ("v", u // 4 - 1, 1)) + 1 if u else 0))
                for mt in range(MT):
                    hi = p_hi[:, buf, mt, k * P:(k + 1) * P]
                    lo = p_lo[:, buf, mt, k * P:(k + 1) * P]
                    c = k * (HALF + 1)
                    pe.matmul(o[:, c:c + HALF + 1], hi, v[:, st, mt, h, 0:HALF + 1], start=(mt == 0), stop=False)
                    pe.matmul(o[:, c:c + HALF], hi, v[:, st, mt, h, VL:VL + HALF], start=False, stop=False)
                    last = pe.matmul(o[:, c:c + HALF + 1], lo, v[:, st, mt, h, 0:HALF + 1], start=False,
                                     stop=(mt == MT - 1))
                if k == QT - 1:
                    last.then_inc(o_made.sem, 1)

            def batch(s):
                for p in range(PAIRS):
                    st1, p1 = (p + 1) % 2, (p + 1) % PAIRS
                    queue, next_pair = queue_slots(s, p), s.layer_of(p) is not None
                    for t in range(SLOTS):
                        T = p * SLOTS + t
                        scores(s, T)
                        for n in max_uses(s, p, t):
                            if n == N_B:
                                pe.wait_ge(q_copied.sem, at(q_copied, s, 32 * (p + 1)))
                            if n in (N_B, N_B + MT):
                                item = ("qk", p, 2 + (n - N_B) // MT)
                                pe.wait_ge(g_free.sem, at(g_free, s, index(s, item) + 1))
                            max_use(s, p * N_MAX, n, p % 2 if n < N_B else st1)
                        if t in QK_SLOTS and next_pair:
                            n = t - QK_SLOTS[0]
                            k0, k1 = 4 * (n % 3), 4 * (n % 3) + 4
                            if p == PAIRS - 1 and n < 3:
                                kt = (k1 - 1) // 3
                                pe.wait_ge(x_low.sem, at(x_low, s, kt + 1))
                                if s.name in QKV_STAGES:
                                    pe.wait_ge(w_low.sem, at(w_low, s, kt + 1))
                            products(s, ("qk", p, n // 3), k0, k1, p1)
                        if t == NORM_SLOT and s.finish == 0 and p in (1, 2):
                            average(s, p - 1)
                        if t in TURN_SLOTS and (p or s.finish is not None):
                            turn_output(s, (p - 1) % PAIRS, TURN_SLOTS[t])
                        for item, k0, k1 in queue.get(t, []):
                            if item == ("proj", 0, 0) and k0 == 0:
                                pe.wait_ge(w_low.sem, at(w_low, s, 0))
                            products(s, item, k0, k1, p1)
                        u = T // MT - 1
                        if T % MT in PV_OFFSETS and (u >= 0 or s.finish is not None):
                            weighted_sum(s, u, PV_OFFSETS[T % MT])

            for kt in range(CT):
                pe.wait_ge(w_low.sem, at(w_low, LEAD, kt + 1))
                pe.wait_ge(x_low.sem, at(x_low, LEAD, kt + 1))
                products(LEAD, ("qk", -1, 0), 3 * kt, 3 * kt + 3)
            for k in range(1, 4):
                products(LEAD, ("qk", -1, k))
            pe.wait_ge(q_copied.sem, at(q_copied, LEAD, 32))
            pe.wait_ge(g_free.sem, at(g_free, LEAD, index(LEAD, ("qk", -1, 3)) + 1))
            pe.wait_ge(const_ready, 1)
            for n in range(N_B, N_MAX):
                max_use(LEAD, -N_B, n, 0)
                k = n - N_B
                if k < 16:
                    products(LEAD, ("v", -1, k // 8), 6 * (k % 8), 6 * (k % 8) + 6)
            pe.wait_ge(w_low.sem, at(w_low, LEAD, 2 * CT))
            batch(FIRST0)
            with pe.Fori(1, NB - 1) as b:
                batch(middle(0, b))
            batch(LAST0)
            batch(FIRST1)
            with pe.Fori(1, NB - 1) as b:
                batch(middle(1, b))
            batch(LAST1)
            for k in range(QT):
                weighted_sum(TAIL, -1, k)
            for half in range(2):
                turn_output(TAIL, PAIRS - 1, half)
            pe.wait_ge(g_free.sem, at(g_free, TAIL, index(TAIL, ("turn", PAIRS - 1, 1)) + 1))
            for ot in range(CT):
                for nh in range(NH):
                    products(TAIL, ("proj", ot, nh))

        @block.scalar
        def _(act):
            def high(s, item, p1, st):
                what, a, n = item
                layer = layer_of(s, item)
                act.wait_ge(g_made.sem, at(g_made, s, index(s, item) + 1))
                g = bank_of(s, item)
                cols = slice((n % 2) * COLS, (n % 2 + 1) * COLS)
                if what == "qk":
                    c = (n // 2) * CT + p1
                    for h in range(2):
                        last = act.activation((qa, ka)[n // 2][own(h), st, h, cols], g[own(h), :], ACT.Identity,
                                              bias=biases[own(h), layer, c:c + 1])
                elif what == "v":
                    last = act.activation(v[:, st, 4 * n:4 * n + 4, :, 0:HALF],
                                          g[:, :].rearrange("p (m h d) -> p m h d", m=4, h=2), ACT.Copy)
                elif what == "turn":
                    last = act.activation(o_hi[:, a, cols], g[:, :], ACT.Identity,
                                          bias=biases[:, layer, 2 * CT + a:2 * CT + a + 1])
                else:
                    last = act.activation(yb[:, a, cols], g[:, :], ACT.Identity,
                                          bias=biases[:, layer, 3 * CT + a:3 * CT + a + 1],
                                          scale=1.0 / WEIGHT_SCALE ** 2)
                last.then_inc(g_high.sem, 1)

            def weights_high(s, loaded, target, source):
                act.wait_ge(loaded.sem, at(loaded, s, 16))
                act.activation(target, source, ACT.Copy, scale=WEIGHT_SCALE).then_inc(w_high.sem, 1)

            def apply_norm(s, ot):
                if ot == 0:
                    act.wait_ge(norm_ready.sem, at(norm_ready, s, 1))
                act.activation(yb[:, ot, :], yb[:, ot, :], ACT.Identity, bias=norm_b[:, ot:ot + 1],
                               scale=norm_a[:, ot:ot + 1]).then_inc(y_scaled.sem, 1)

            def exps(s, T):
                u, j = T // MT, T // 2
                act.wait_ge(s_made.sem, at(s_made, s, T + 1))
                if T % MT == 0 and (s.name != "first0" or u >= 2):
                    act.wait_ge(o_made.sem, at(o_made, s, u - 1))
                if T % 2 == 0 and (s.name != "first0" or j >= RING):
                    act.wait_ge(p_rest.sem, at(p_rest, s, j - RING + 1))
                bank = s_bank[T % 2]
                act.activation(p_f32[:, j % RING, T % 2, :], bank[:, :], ACT.Exp, scale=EXP_SCALE)
                act.activation(p_hi[:, u % 2, T % MT, :], bank[:, :], ACT.Exp, scale=EXP_SCALE).then_inc(p_made.sem, 1)

            def batch(s):
                for p in range(PAIRS):
                    evict = evictions(s, p)
                    for t in range(SLOTS):
                        T = p * SLOTS + t
                        for item in evict[t]:
                            if item == ("proj", 0, 0):
                                act.wait_ge(y_stored.sem, at(y_stored, s, 0))
                            high(s, item, (p + 1) % PAIRS, (p + 1) % 2)
                        if p == NEXT_X_PAIR and t in WEIGHT_SLOTS and s.name in QKV_STAGES:
                            kt = WEIGHT_SLOTS[t]
                            if kt == 0:
                                act.wait_ge(g_made.sem, at(g_made, s, index(s, ("v", p, 1)) + 1))
                            weights_high(s, w_loaded[kt], w_hi[:, kt, 0:3 * C], w_in[kt])
                        if p == PAIRS - 1 and t in PROJ_WEIGHT_SLOTS and s.name in PROJ_STAGES:
                            kt = PROJ_WEIGHT_SLOTS[t]
                            weights_high(s, w_loaded[kt], w_hi[:, kt, 3 * C:4 * C], yb[:, kt, 0:C])
                        if T - SLOTS in APPLY_SLOTS and s.finish == 0:
                            apply_norm(s, APPLY_SLOTS[T - SLOTS])
                        exps(s, T)

            for kt in range(CT):
                weights_high(LEAD, w_loaded[kt], of_pairs(w_hi[:, kt, :], 0, 1), of_pairs(w_in[kt], 0, 1))
            act.wait_ge(const_ready, 1)
            act.wait_ge(params_ready, 1)
            for n, item in enumerate(ORDER["lead"]):
                high(LEAD, item, 0, 0)
                if n < CT:
                    weights_high(LEAD, others_loaded[n], of_pairs(w_hi[:, n, :], 1, PAIRS), of_pairs(w_in[n], 1, PAIRS))
            batch(FIRST0)
            with act.Fori(1, NB - 1) as b:
                batch(middle(0, b))
            batch(LAST0)
            batch(FIRST1)
            with act.Fori(1, NB - 1) as b:
                batch(middle(1, b))
            batch(LAST1)
            act.wait_ge(y_stored.sem, at(y_stored, TAIL, 0))
            for item in ORDER["tail"]:
                high(TAIL, item, 0, 0)

        @block.vector
        def _(dve):
            def low(s, item, p1, st):
                what, a, n = item
                layer = layer_of(s, item)
                dve.wait_ge(g_high.sem, at(g_high, s, high_index(s, item) + 1))
                g = bank_of(s, item)
                cols = slice((n % 2) * COLS, (n % 2 + 1) * COLS)
                if what == "qk":
                    c = (n // 2) * CT + p1
                    upper, lower = ((qa, qb), (ka, ka))[n // 2]
                    for h in range(2):
                        rows = own(h) if n < 2 else own(1 - h)
                        last = dve.scalar_tensor_tensor(out=lower[rows, st, h, cols], in0=g[own(h), :],
                                                        scalar=biases[own(h), layer, c:c + 1],
                                                        in1=upper[own(h), st, h, cols], op0=ALU.add, op1=ALU.subtract)
                elif what == "v":
                    last = dve.tensor_tensor(v[:, st, 4 * n:4 * n + 4, :, VL:VL + HALF],
                                             g[:, :].rearrange("p (m h d) -> p m h d", m=4, h=2),
                                             v[:, st, 4 * n:4 * n + 4, :, 0:HALF], ALU.subtract)
                elif what == "turn":
                    last = dve.scalar_tensor_tensor(out=o_lo[:, a, cols], in0=g[:, :],
                                                    scalar=biases[:, layer, 2 * CT + a:2 * CT + a + 1],
                                                    in1=o_hi[:, a, cols], op0=ALU.add, op1=ALU.subtract)
                elif layer == 0:
                    last = dve.bn_stats(bn[:, a, n, :], yb[:, a, cols])
                else:
                    if a == 0 and n == 0:
                        dve.wait_ge(res_loaded.sem, at(res_loaded, s, 0))
                    dve.tensor_tensor(yb[:, a, cols], yb[:, a, cols], x_res[:, a, cols], ALU.add)\
                        .then_inc(res_added.sem, 1)
                    last = dve.engine_nop()
                last.then_inc(g_free.sem, 1)

            def max_read_out(s, n0, n):
                h, k = MAX_ORDER[n]
                dve.wait_ge(max_made.sem, at(max_made, s, n0 + n + 1))
                m = m_bank[n % 2]
                if k is None:
                    dve.tensor_copy(shift_rows[:, h, :], m[0:MT, 0:HALF].bitcast(F16)).then_inc(max_read.sem, 1)
                else:
                    dve.tensor_reduce(maxes[:, h, k:k + 1], m[:, :], AX.X, ALU.max).then_inc(max_read.sem, 1)

            def make_shift(s, n0, h):
                n = N_B - 1 if h else N_MAX - 1
                dve.wait_ge(max_read.sem, at(max_read, s, n0 + n))
                dve.tensor_tensor(row_max[:, h, :], maxes[:, h, 0:MT], maxes[:, h, MT:2 * MT], ALU.max)\
                    .then_inc(max_joined.sem, 1)
                dve.wait_ge(max_joined.sem, at(max_joined, s, shifts_until(n0, h)))
                dve.tensor_scalar(shift[:, h, :], row_max[:, h, :], -1.0 / SHIFT_UNIT, SHIFT_BONUS, ALU.mult, ALU.add)\
                    .then_inc(shift_ready.sem, 1)

            def divide(s, u):
                h, nh = (u // 2) % 2, u % 2
                dve.wait_ge(o_made.sem, at(o_made, s, u + 1))
                if u % 4 == 0 and u:
                    dve.wait_ge(g_made.sem, at(g_made, s, index(s, ("turn", u // 4 - 1, 1)) + 1))
                if u == 0 and s.finish is not None:
                    dve.wait_ge(g_made.sem, at(g_made, s, index(s, ("turn", PAIRS - 1, 1)) + 1))
                o = o_bank[u % 2][:, 0:QT * (HALF + 1)].rearrange("p (q d) -> p q d", d=HALF + 1)
                dve.reciprocal(recip[:, u % 2, :], o[:, :, HALF]).then_inc(o_recip.sem, 1)
                dve.wait_ge(o_recip.sem, at(o_recip, s, u + 1))
                dve.tensor_tensor(o_pair[:, nh * QT:(nh + 1) * QT, own(h)], o[:, :, 0:HALF],
                                  recip[:, u % 2, :].unsqueeze(2).to_broadcast([P, QT, HALF]), ALU.mult)\
                    .then_inc(o_read.sem, 1)

            def x_normalise(s, kt):
                a, b = (t[:, one(s.following), kt:kt + 1].rearrange("p b o -> p (b o)") for t in (next_a, next_b))
                dve.wait_ge(x_loaded[kt].sem, at(x_loaded[kt], s, 16))
                dve.wait_ge(norm_ready.sem, at(norm_ready, s, 0))
                dve.tensor_scalar(x_in[:, kt, :], x_in[:, kt, :], a, b, ALU.mult, ALU.add).then_inc(x_normed.sem, 1)

            def x_round(s, kt):
                if s.ahead == 0:
                    dve.wait_ge(x_loaded[kt].sem, at(x_loaded[kt], s, 16))
                else:
                    dve.wait_ge(x_normed.sem, at(x_normed, s, kt + 1))
                dve.tensor_copy(x_hi[:, kt, :], x_in[:, kt, :]).then_inc(x_high.sem, 1)

            def x_rest(s, kt):
                dve.wait_ge(x_high.sem, at(x_high, s, kt + 1))
                dve.tensor_tensor(x_lo[:, kt, :], x_in[:, kt, :], x_hi[:, kt, :], ALU.subtract).then_inc(x_low.sem, 1)

            class Norm:

                def __init__(self, s):
                    self.s, self.n = s, 0

                def link(self, ins):
                    self.n += 1
                    ins.then_inc(links.sem, 1)
                    dve.wait_ge(links.sem, at(links, self.s, self.n))

                def moments(self, which):
                    s = self.s
                    if which == 0:
                        dve.wait_ge(g_free.sem, at(g_free, s, index(s, ("proj", CT - 1, NH - 1)) + 1))
                    dve.memset(tmp[:, :], 0.0)
                    for ot in range(CT):
                        last = dve.bn_aggr(mv[:, ot, :], bn[:, ot, :, :].rearrange("p a s -> p (a s)"))
                    self.link(last)
                    dve.tensor_copy(gs[:, 0:CT], mv[:, :, 0])
                    self.link(dve.tensor_tensor(tmp[:, :], mv[:, :, 0], mv[:, :, 0], ALU.mult))
                    dve.tensor_tensor(gs[:, CT:2 * CT], tmp[:, :], mv[:, :, 1], ALU.add).then_inc(stats_ready.sem, 1)

                def variance(self, which):
                    s = self.s
                    item = ("norm", which, 0)
                    dve.wait_ge(g_made.sem, at(g_made, s, index(s, item) + 1))
                    dve.tensor_copy(gm[:, :], bank_of(s, item)[:, 0:2 * CT]).then_inc(g_free.sem, 1)
                    dve.wait_ge(g_free.sem, at(g_free, s, index(s, item) + 1))
                    self.link(dve.tensor_tensor(tmp[:, :], gm[:, 0:CT], gm[:, 0:CT], ALU.mult))
                    self.link(dve.scalar_tensor_tensor(out=tmp[:, :], in0=gm[:, CT:2 * CT], scalar=1.0, in1=tmp[:, :],
                                                       op0=ALU.mult, op1=ALU.subtract))
                    dve.tensor_scalar(var[:, :], tmp[:, :], EPS, None, ALU.add).then_inc(var_ready.sem, 1)

                def factors(self, which):
                    a_out, b_out = (norm_a[:, :], norm_b[:, :]) if which == 0 else \
                        (t[:, one(self.s.before), :].rearrange("p b o -> p (b o)") for t in (next_a, next_b))
                    dve.wait_ge(rstd_ready.sem, at(rstd_ready, self.s, which + 1))
                    self.link(dve.tensor_tensor(a_out, rstd[:, :], affine[:, 2 * which, :], ALU.mult))
                    self.link(dve.tensor_tensor(tmp[:, :], gm[:, 0:CT], a_out, ALU.mult))
                    dve.tensor_tensor(b_out, affine[:, 2 * which + 1, :], tmp[:, :], ALU.subtract).then_inc(norm_ready.sem, 1)

                def add(self, ot):
                    s = self.s
                    if ot == 0:
                        dve.wait_ge(res_loaded.sem, at(res_loaded, s, 0))
                    dve.wait_ge(y_scaled.sem, at(y_scaled, s, ot + 1))
                    dve.tensor_tensor(yb[:, ot, :], yb[:, ot, :], x_res[:, ot, :], ALU.add).then_inc(res_added.sem, 1)
                    dve.wait_ge(res_added.sem, at(res_added, s, ot + 1))
                    for nh in range(NH):
                        last = dve.bn_stats(bn[:, ot, nh, :], yb[:, ot, nh * COLS:(nh + 1) * COLS])
                    if ot == CT - 1:
                        self.link(last)

            def weights_rest(s, n, low_half, high_half, source):
                dve.wait_ge(w_high.sem, at(w_high, s, n + 1))
                dve.scalar_tensor_tensor(out=low_half, in0=source, scalar=WEIGHT_SCALE, in1=high_half,
                                         op0=ALU.mult, op1=ALU.subtract).then_inc(w_low.sem, 1)

            def batch(s):
                norm = Norm(s)
                for p in range(PAIRS):
                    evict = evictions(s, p)
                    for t in range(SLOTS):
                        T = p * SLOTS + t
                        if t == SHIFT_A_CHAIN and s.layer_of(p) is not None:
                            make_shift(s, p * N_MAX, 0)
                        if t == SHIFT_B_CHAIN:
                            make_shift(s, p * N_MAX, 1)
                        for n in max_uses(s, p, t):
                            max_read_out(s, p * N_MAX, n)
                        if T % MT == 0 and (T >= 2 * MT or s.finish is not None):
                            divide(s, T // MT - 2)
                        for item in evict[t]:
                            low(s, item, (p + 1) % PAIRS, (p + 1) % 2)
                        if p == NEXT_X_PAIR and s.ahead is not None:
                            if t in NORMALISE_SLOTS and s.ahead == 1:
                                x_normalise(s, NORMALISE_SLOTS[t])
                            if t - 1 in WEIGHT_SLOTS and s.name in QKV_STAGES:
                                kt = WEIGHT_SLOTS[t - 1]
                                weights_rest(s, kt, w_lo[:, kt, 0:3 * C], w_hi[:, kt, 0:3 * C], w_in[kt])
                        since = T - NEXT_X_PAIR * SLOTS
                        if since == min(NEXT_X_SLOTS) and s.ahead is not None:
                            dve.wait_ge(g_made.sem, at(g_made, s, index(s, ("v", p, 1)) + 1))
                        if since in NEXT_X_SLOTS and s.ahead is not None:
                            x_round(s, NEXT_X_SLOTS[since])
                        if since - 1 in NEXT_X_SLOTS and s.ahead is not None:
                            x_rest(s, NEXT_X_SLOTS[since - 1])
                        if p == PAIRS - 1 and t - 1 in PROJ_WEIGHT_SLOTS and s.name in PROJ_STAGES:
                            kt = PROJ_WEIGHT_SLOTS[t - 1]
                            weights_rest(s, kt, w_lo[:, kt, 3 * C:4 * C], w_hi[:, kt, 3 * C:4 * C], yb[:, kt, 0:C])
                        if s.finish == 0 and p in (1, 2):
                            if t == STATS_SLOTS[p - 1]:
                                norm.moments(p - 1)
                            if t == VAR_SLOT:
                                norm.variance(p - 1)
                            if t == FACTOR_SLOT:
                                norm.factors(p - 1)
                            if T - SLOTS - 1 in APPLY_SLOTS:
                                norm.add(APPLY_SLOTS[T - SLOTS - 1])
                assert norm.n == links.counts[s.name], norm.n

            for kt in range(CT):
                x_round(LEAD, kt)
                weights_rest(LEAD, kt, *(of_pairs(t, 0, 1) for t in (w_lo[:, kt, :], w_hi[:, kt, :], w_in[kt])))
                x_rest(LEAD, kt)
            dve.wait_ge(const_ready, 1)
            dve.wait_ge(params_in, 96)
            dve.tensor_scalar(biases[:, 1, 0:3 * CT], biases[:, 1, 0:3 * CT], WEIGHT_SCALE, None, ALU.mult)\
                .then_inc(params_ready, 1)
            dve.wait_ge(params_ready, 1)
            dve.engine_nop().then_inc(y_stored.sem, 1)
            for k in range(4):
                low(LEAD, ("qk", -1, k), 0, 0)
                weights_rest(LEAD, CT + k, *(of_pairs(t, 1, PAIRS) for t in (w_lo[:, k, :], w_hi[:, k, :], w_in[k])))
            for n in range(N_B, N_MAX):
                if n == N_MAX - 1:
                    make_shift(LEAD, -N_B, 0)
                max_read_out(LEAD, -N_B, n)
            for nh in range(2):
                low(LEAD, ("v", -1, nh), 0, 0)
            batch(FIRST0)
            with dve.Fori(1, NB - 1) as b:
                batch(middle(0, b))
            batch(LAST0)
            batch(FIRST1)
            with dve.Fori(1, NB - 1) as b:
                batch(middle(1, b))
            batch(LAST1)
            divide(TAIL, -2)
            divide(TAIL, -1)
            for item in ORDER["tail"]:
                low(TAIL, item, 0, 0)


_INS = ["x", "L0_conv_w_qkv", "L0_conv_w_proj", "L0_conv_gamma", "L0_conv_beta", "L1_conv_norm_w", "L1_conv_norm_b",
        "L1_conv_qkv_w", "L1_conv_qkv_b", "L1_conv_proj_w", "L1_conv_proj_b"]
_TURNED = {"L0_conv_w_qkv", "L0_conv_w_proj", "L1_conv_qkv_w", "L1_conv_proj_w"}


def kernel(**inputs):
    import numpy as _np
    import concourse.bacc as _bacc
    from concourse import mybir as _mybir
    from concourse.bass_utils import run_bass_kernel_spmd as _run

    nc = _bacc.Bacc("TRN2", target_bir_lowering=False, num_devices=1)
    arrays, args = {}, []
    for name in _INS:
        a = _np.asarray(inputs[name])
        if name == "x":
            b, c, h, w = a.shape
            a = a.reshape(b, c, h * w)
        if name in _TURNED:
            a = a.T
        if a.ndim == 1:
            a = a.reshape(-1, 128).T
        a = _np.ascontiguousarray(a)
        arrays[f"in_{name}_dram"] = a
        args.append(nc.dram_tensor(f"in_{name}_dram", a.shape, _mybir.dt.from_np(a.dtype), kind="ExternalInput").ap())
    args.append(nc.dram_tensor("out_0_dram", (b, c, h * w), _mybir.dt.float32, kind="ExternalOutput").ap())
    two_attention_blocks(nc, *args)
    r = _run(nc, [arrays], core_ids=[0])
    return _np.asarray(r.results[0]["out_0_dram"]).reshape(b, c, h, w)
```
